# Optimizing a Trainium2 kernel written in Bass

```python
import numpy as np
import jax
import jax.numpy as jnp

def _softmax(x, axis=-1):
    return jax.nn.softmax(x, axis=axis)

def _gelu(x):
    return jax.nn.gelu(x, approximate=True)

def _silu(x):
    return jax.nn.silu(x)

def _sigmoid(x):
    return jax.nn.sigmoid(x)

def _layernorm(x, axis=-1, eps=1e-05):
    m = jnp.mean(x, axis=axis, keepdims=True)
    v = jnp.var(x, axis=axis, keepdims=True)
    return (x - m) / jnp.sqrt(v + eps)

def _scatter_add(tgt, idx, src, axis=0):
    return tgt.at[idx].add(src)

def _segment_sum(src, seg, n):
    return jax.ops.segment_sum(src, seg, n)
kernel_name = 'mk_flamingo_gated_d1_seqx_r4_3920bf'

def setup_inputs(seed: int=0):
    np.random.seed(seed)
    _w = jnp.asarray

    def _rec_inputs():
        import jax
        import jax.numpy as jnp
        _rk = jax.random.key(seed)
        x = 7.22e-05 + 1 * jax.random.normal(jax.random.fold_in(_rk, 1), (8, 100, 512), jnp.float32)
        _lenS = 100 - jax.random.randint(jax.random.fold_in(_rk, 7), (8,), 0, max(1, 100 // 4) + 1, jnp.int32)
        _lenS2 = 361 - jax.random.randint(jax.random.fold_in(_rk, 8), (8,), 0, max(1, 361 // 4) + 1, jnp.int32)
        _ctx_2048P = jax.random.normal(jax.random.fold_in(_rk, 11), (8, 16, 512), jnp.float32)
        _ctx_2048c = jax.random.dirichlet(jax.random.fold_in(_rk, 511), 0.3 * jnp.ones((16,), jnp.float32), (8, 361))
        _ctx_2048t = jnp.einsum('bsk,bkd->bsd', _ctx_2048c, _ctx_2048P)
        _ctx_2048t = _ctx_2048t * jax.lax.rsqrt(jnp.mean(jnp.square(_ctx_2048t)) + 1e-12) * 0.953939
        ctx_2048 = -0.000514642 + 1.00011 * (_ctx_2048t + 0.3 * jax.random.normal(jax.random.fold_in(_rk, 611), (8, 361, 512), jnp.float32))
        _g = jax.random.normal(jax.random.fold_in(_rk, 9001), (2, 1), jnp.float32)
        _g = jnp.sign(_g) * jnp.maximum(jnp.abs(_g), 1.0) + (_g == 0) * 1.0
        g_xattn = _g[0]
        g_ffn = _g[1]
        return (x, ctx_2048, g_xattn, g_ffn)
    x, ctx_2048, g_xattn, g_ffn = _rec_inputs()

    def _L0_xattn_setup():
        import jax, jax.numpy as jnp
        import numpy as np
        D_MODEL = 512
        NUM_HEADS = 16
        HEAD_DIM = D_MODEL // NUM_HEADS

        def _fq_sym(x, axis):
            s = jnp.max(jnp.abs(x), axis=axis, keepdims=True) / 127.0
            s = jnp.maximum(s, 1e-08)
            q = jnp.clip(jnp.round(x / s), -127.0, 127.0) * s
            return x + jax.lax.stop_gradient(q - x)

        def _fq_unsigned(x, axis):
            s = jnp.max(x, axis=axis, keepdims=True) / 255.0
            s = jnp.maximum(s, 1e-08)
            q = jnp.clip(jnp.round(x / s), 0.0, 255.0) * s
            return x + jax.lax.stop_gradient(q - x)
        key = jax.random.key(seed)
        ks = jax.random.split(key, 8)
        B, N, M, C = (2, 512, 128, D_MODEL)
        return {'x': jax.random.normal(ks[0], (B, N, C), jnp.float32), 'cond': jax.random.normal(ks[1], (B, M, C), jnp.float32), 'Wq': jax.random.normal(ks[2], (C, C), jnp.float32) * 0.02, 'bq': jnp.zeros((C,), jnp.float32), 'Wkv': jax.random.normal(ks[3], (C, 2 * C), jnp.float32) * 0.02, 'bkv': jnp.zeros((2 * C,), jnp.float32), 'Wp': jax.random.normal(ks[4], (C, C), jnp.float32) * 0.02, 'bp': jnp.zeros((C,), jnp.float32)}
    _L0_xattn_all = _L0_xattn_setup()
    _L0_xattn_in = {k: v for k, v in _L0_xattn_all.items() if k in ('Wq', 'bq', 'Wkv', 'bkv', 'Wp', 'bp')}
    del _L0_xattn_all

    def _L0_ffn_setup():
        import jax, jax.numpy as jnp
        import numpy as np
        DIM = 512
        INTER = 352
        E = 16
        TOPK = 4
        G = 4
        TOPK_G = 2
        N_SHARED = 2
        SHARED_INTER = N_SHARED * INTER
        ROUTE_SCALE = 1.0

        def _moe_forward(x, Wg, W1, W3, W2, Ws1, Ws3, Ws2):
            B, S, D = x.shape
            xt = x.reshape(-1, D)
            T = xt.shape[0]
            scores = jax.nn.softmax(xt @ Wg.T, axis=-1)
            sg = scores.reshape(T, G, E // G)
            group_scores = sg.max(axis=-1)
            gidx = jax.lax.top_k(group_scores, TOPK_G)[1]
            gmask = jax.nn.one_hot(gidx, G, dtype=jnp.float32).sum(axis=1) > 0
            masked = jnp.where(gmask[:, :, None], sg, -jnp.inf).reshape(T, E)
            topi = jax.lax.top_k(masked, TOPK)[1]
            weights = jnp.take_along_axis(scores, topi, axis=1) * ROUTE_SCALE
            combine = jnp.zeros((T, E), xt.dtype).at[jnp.arange(T)[:, None], topi].add(weights)
            h = jax.nn.silu(jnp.einsum('td,eid->eti', xt, W1)) * jnp.einsum('td,eid->eti', xt, W3)
            expert_out = jnp.einsum('eti,edi->etd', h, W2)
            y = jnp.einsum('etd,te->td', expert_out, combine)
            z = jax.nn.silu(xt @ Ws1.T) * (xt @ Ws3.T) @ Ws2.T
            return (y + z).reshape(B, S, D)
        key = jax.random.key(seed)
        ks = jax.random.split(key, 8)
        s = 0.02
        x = jax.random.normal(ks[0], (1, 512, DIM), dtype=jnp.float32)
        Wg = jax.random.normal(ks[1], (E, DIM), dtype=jnp.float32) * s
        W1 = jax.random.normal(ks[2], (E, INTER, DIM), dtype=jnp.float32) * s
        W3 = jax.random.normal(ks[3], (E, INTER, DIM), dtype=jnp.float32) * s
        W2 = jax.random.normal(ks[4], (E, DIM, INTER), dtype=jnp.float32) * s
        Ws1 = jax.random.normal(ks[5], (SHARED_INTER, DIM), dtype=jnp.float32) * s
        Ws3 = jax.random.normal(ks[6], (SHARED_INTER, DIM), dtype=jnp.float32) * s
        Ws2 = jax.random.normal(ks[7], (DIM, SHARED_INTER), dtype=jnp.float32) * s
        return {'x': x, 'Wg': Wg, 'W1': W1, 'W3': W3, 'W2': W2, 'Ws1': Ws1, 'Ws3': Ws3, 'Ws2': Ws2}
    _L0_ffn_all = _L0_ffn_setup()
    _L0_ffn_in = {k: v for k, v in _L0_ffn_all.items() if k in ('Wg', 'W1', 'W3', 'W2', 'Ws1', 'Ws3', 'Ws2')}
    del _L0_ffn_all
    return {'x': x, 'ctx_2048': ctx_2048, 'g_xattn': g_xattn, 'g_ffn': g_ffn, 'L0_xattn_Wq': _L0_xattn_in['Wq'], 'L0_xattn_bq': _L0_xattn_in['bq'], 'L0_xattn_Wkv': _L0_xattn_in['Wkv'], 'L0_xattn_bkv': _L0_xattn_in['bkv'], 'L0_xattn_Wp': _L0_xattn_in['Wp'], 'L0_xattn_bp': _L0_xattn_in['bp'], 'L0_ffn_Wg': _L0_ffn_in['Wg'], 'L0_ffn_W1': _L0_ffn_in['W1'], 'L0_ffn_W3': _L0_ffn_in['W3'], 'L0_ffn_W2': _L0_ffn_in['W2'], 'L0_ffn_Ws1': _L0_ffn_in['Ws1'], 'L0_ffn_Ws3': _L0_ffn_in['Ws3'], 'L0_ffn_Ws2': _L0_ffn_in['Ws2']}

def reference(x, ctx_2048, g_xattn, g_ffn, L0_xattn_Wq, L0_xattn_bq, L0_xattn_Wkv, L0_xattn_bkv, L0_xattn_Wp, L0_xattn_bp, L0_ffn_Wg, L0_ffn_W1, L0_ffn_W3, L0_ffn_W2, L0_ffn_Ws1, L0_ffn_Ws3, L0_ffn_Ws2):
    import jax
    import jax.numpy as jnp

    def _L0_xattn_ref(x, cond, Wq, bq, Wkv, bkv, Wp, bp):
        import jax, jax.numpy as jnp
        import numpy as np
        D_MODEL = 512
        NUM_HEADS = 16
        HEAD_DIM = D_MODEL // NUM_HEADS

        def _fq_sym(x, axis):
            s = jnp.max(jnp.abs(x), axis=axis, keepdims=True) / 127.0
            s = jnp.maximum(s, 1e-08)
            q = jnp.clip(jnp.round(x / s), -127.0, 127.0) * s
            return x + jax.lax.stop_gradient(q - x)

        def _fq_unsigned(x, axis):
            s = jnp.max(x, axis=axis, keepdims=True) / 255.0
            s = jnp.maximum(s, 1e-08)
            q = jnp.clip(jnp.round(x / s), 0.0, 255.0) * s
            return x + jax.lax.stop_gradient(q - x)
        B, N, C = x.shape
        H, hd = (NUM_HEADS, HEAD_DIM)
        q = (x @ Wq + bq).reshape(1, B * N, H, hd)
        kv = (cond @ Wkv + bkv).reshape(1, -1, 2, H, hd)
        k, v = (kv[:, :, 0], kv[:, :, 1])
        scale = 1.0 / np.sqrt(hd).astype(np.float32)
        q = jnp.transpose(q * scale, (0, 2, 1, 3))
        k = jnp.transpose(k, (0, 2, 1, 3))
        v = jnp.transpose(v, (0, 2, 1, 3))
        q = _fq_sym(q, axis=-1)
        k = _fq_sym(k, axis=-1)
        v = _fq_sym(v, axis=2)
        attn = jnp.einsum('bhqd,bhkd->bhqk', q, k)
        attn = jax.nn.softmax(attn.astype(jnp.float32), axis=-1)
        attn = _fq_unsigned(attn, axis=-1)
        out = jnp.einsum('bhqk,bhkd->bhqd', attn, v)
        out = jnp.transpose(out, (0, 2, 1, 3)).reshape(B, N, C)
        return out @ Wp + bp

    def _L0_ffn_ref(x, Wg, W1, W3, W2, Ws1, Ws3, Ws2):
        import jax, jax.numpy as jnp
        import numpy as np
        DIM = 512
        INTER = 352
        E = 16
        TOPK = 4
        G = 4
        TOPK_G = 2
        N_SHARED = 2
        SHARED_INTER = N_SHARED * INTER
        ROUTE_SCALE = 1.0

        def _moe_forward(x, Wg, W1, W3, W2, Ws1, Ws3, Ws2):
            B, S, D = x.shape
            xt = x.reshape(-1, D)
            T = xt.shape[0]
            scores = jax.nn.softmax(xt @ Wg.T, axis=-1)
            sg = scores.reshape(T, G, E // G)
            group_scores = sg.max(axis=-1)
            gidx = jax.lax.top_k(group_scores, TOPK_G)[1]
            gmask = jax.nn.one_hot(gidx, G, dtype=jnp.float32).sum(axis=1) > 0
            masked = jnp.where(gmask[:, :, None], sg, -jnp.inf).reshape(T, E)
            topi = jax.lax.top_k(masked, TOPK)[1]
            weights = jnp.take_along_axis(scores, topi, axis=1) * ROUTE_SCALE
            combine = jnp.zeros((T, E), xt.dtype).at[jnp.arange(T)[:, None], topi].add(weights)
            h = jax.nn.silu(jnp.einsum('td,eid->eti', xt, W1)) * jnp.einsum('td,eid->eti', xt, W3)
            expert_out = jnp.einsum('eti,edi->etd', h, W2)
            y = jnp.einsum('etd,te->td', expert_out, combine)
            z = jax.nn.silu(xt @ Ws1.T) * (xt @ Ws3.T) @ Ws2.T
            return (y + z).reshape(B, S, D)
        return _moe_forward(x, Wg, W1, W3, W2, Ws1, Ws3, Ws2)
    x = x + jnp.tanh(g_xattn[0]) * _L0_xattn_ref(_layernorm(x, axis=-1), ctx_2048, L0_xattn_Wq, L0_xattn_bq, L0_xattn_Wkv, L0_xattn_bkv, L0_xattn_Wp, L0_xattn_bp)
    x = x + jnp.tanh(g_ffn[0]) * _L0_ffn_ref(_layernorm(x, axis=-1), L0_ffn_Wg, L0_ffn_W1, L0_ffn_W3, L0_ffn_W2, L0_ffn_Ws1, L0_ffn_Ws3, L0_ffn_Ws2)
    return x

_drawn_inputs = setup_inputs


def setup_inputs(seed=0):
    import zlib

    import numpy as np

    out = dict(_drawn_inputs(seed))
    spreads = {'L0_xattn_bq': (0.0, 2.0), 'L0_xattn_bkv': (0.0, 0.1), 'L0_xattn_bp': (0.0, 0.1)}
    factors = {'L0_xattn_Wq': 8.0,
     'L0_ffn_Wg': 7.315,
     'L0_ffn_W1': 6.132,
     'L0_ffn_W3': 6.106,
     'L0_ffn_W2': 6.09,
     'L0_ffn_Ws1': 8.0,
     'L0_ffn_Ws3': 8.0,
     'L0_ffn_Ws2': 8.0}
    for name, (base, spread) in spreads.items():
        noise = np.random.default_rng([zlib.crc32(name.encode()), seed]).standard_normal(out[name].shape)
        drawn = base * np.exp(spread * noise) if base else spread * noise
        out[name] = jnp.asarray(drawn.astype(out[name].dtype))
    for name, factor in factors.items():
        out[name] = (out[name] * factor).astype(out[name].dtype)
    return out
```

```python
import math
from contextlib import ExitStack

import concourse.bass as bass
from concourse import mybir


def gated_xattn_moe_kernel(
    nc: bass.Bass,
    x: bass.AP,
    ctx_t: bass.AP,
    g_xattn: bass.AP,
    g_ffn: bass.AP,
    wq: bass.AP,
    bq: bass.AP,
    wkv: bass.AP,
    bkv: bass.AP,
    wp: bass.AP,
    bp: bass.AP,
    wg_t: bass.AP,
    w_up: bass.AP,
    w_down: bass.AP,
    out: bass.AP,
):
    f32, bf16, i16 = mybir.dt.float32, mybir.dt.bfloat16, mybir.dt.int16
    ALU, ACT, AX = mybir.AluOpType, mybir.ActivationFunctionType, mybir.AxisListType

    P = 128
    NTOK, D = x.shape
    DC = D // P
    NKEY = ctx_t.shape[2]
    H, HD = 16, 32
    HG = P // HD
    NG = H // HG
    T = (NTOK + P - 1) // P
    TAIL = NTOK - (T - 1) * P
    KT = (NKEY + P - 1) // P
    KPAD = KT * P
    E = wg_t.shape[2]
    EX = w_up.shape[0]
    INTER = w_up.shape[2] // (2 * DC)
    IC = w_down.shape[2] // D
    IW = [min(P, INTER - P * c) for c in range(IC)]
    EG, TOPG, TOPK = 4, 2, 4
    LN_EPS = 1e-5
    QSCALE = 1.0 / math.sqrt(HD)
    LOG255 = math.log(255.0)
    BANK = 512

    SPANS = [(0, 512), (512, 512), (1024, 1024), (2048, NKEY - 2048)]
    NS = len(SPANS)
    PIECES = []
    for s, (a, w) in enumerate(SPANS):
        for b in range(a, a + w, BANK):
            e = min(b + BANK, a + w)
            PIECES.append((b, e - b, s if b == a else None, s if e == a + w else None))

    ctx = ExitStack()
    with ctx:
        def sb(name, shape, dt):
            return ctx.enter_context(nc.sbuf_tensor(name, shape, dt))

        def sem(name):
            return ctx.enter_context(nc.semaphore(name))

        key_parts = nc.dram_tensor("key_parts", [KPAD, H * P], bf16, kind="Internal").ap()

        arena_a = sb("arena_a", [P, DC * KPAD], f32)
        arena_b = sb("arena_b", [P, 4608], f32)
        x_sb = sb("x_sb", [P, T, D], f32)
        w_qkv = sb("w_qkv", [P, 3, DC, D], f32)
        bias_rows = sb("bias_rows", [P, 3, D], f32)
        bv_col = sb("bv_col", [P, NG], f32)
        xt = sb("xt", [P, T * D], f32)
        q_t = sb("q_t", [P, H, T * P], bf16)
        v_q = sb("v_q", [P, KT, D], bf16)
        proj_f = sb("proj_f", [P, 2, D], f32)
        proj_i = sb("proj_i", [P, 2, D], i16)
        proj_d = sb("proj_d", [P, 2, D], f32)
        proj_r = sb("proj_r", [P, 2, D], f32)
        parts = sb("parts", [P, 2, H, HG, HD], bf16)
        ident = sb("ident", [P, P], f32)
        gates = sb("gates", [P, 2], f32)
        wg_sb = sb("wg_sb", [P, DC, E], f32)
        stats = sb("stats", [P, T, 6], f32)
        mean_var = sb("mean_var", [P, T, 2], f32)
        std = sb("std", [P, T], f32)
        amax = sb("amax", [P, 2, H], f32)
        step = sb("step", [P, 2, H], f32)
        inv_step = sb("inv_step", [P, 2, H], f32)
        v_amax = sb("v_amax", [P, NG], f32)
        v_step = sb("v_step", [P, NG], f32)
        v_inv = sb("v_inv", [P, NG], f32)
        q_step = sb("q_step", [P, H, T], f32)
        neg_q_step = sb("neg_q_step", [P, H, T], f32)
        span_max = sb("span_max", [P, 2, NS], f32)
        row_max = sb("row_max", [P, 2], f32)
        exp_bias = sb("exp_bias", [P, 2], f32)
        exp_sums = sb("exp_sums", [P, H, T, NS], f32)
        inv_sum = sb("inv_sum", [P, H, T], f32)
        logit = sb("logit", [P, T, E], f32)
        score = sb("score", [P, T, E], f32)
        tok = sb("tok", [P, T], f32)
        grp = sb("grp", [P, T, EG], f32)
        grp_rank = sb("grp_rank", [P, T, EG], f32)
        rank = sb("rank", [P, T, E], f32)
        weight = sb("weight", [P, T, EX], f32)
        before = sb("before", [P, E, E], f32)
        before_g = sb("before_g", [P, EG, EG], f32)

        ps = ctx.enter_context(nc.psum_tensor("ps", [P, 8, BANK], f32))
        ps_flat = ps[:, :, :].rearrange("p b n -> p (b n)")

        ctx_sb = arena_a[:, :].rearrange("p (k n) -> p k n", k=DC)

        def bf_view(a, cols):
            return arena_a[:, a:a + cols // 2].bitcast(bf16)

        half = KPAD // 2
        k_t = [bf_view(half * i, KPAD) for i in range(2)]
        p_int = [arena_a[:, half * (2 + i):half * (3 + i)].bitcast(i16) for i in range(2)]
        p_bf = [bf_view(half * (4 + i), KPAD) for i in range(2)]
        p_t = [bf_view(half * (6 + i), KPAD).rearrange("p (c q) -> p c q", q=P) for i in range(2)]
        UPC, DNC = 2 * DC * INTER, IC * D
        up_sb = [arena_a[:, i * (UPC + DNC):i * (UPC + DNC) + UPC].rearrange("p (w k n) -> p w k n", w=2, k=DC)
                 for i in range(2)]
        down_sb = [arena_a[:, i * (UPC + DNC) + UPC:(i + 1) * (UPC + DNC)].rearrange("p (c n) -> p c n", c=IC)
                   for i in range(2)]
        xn = arena_b[:, 0:T * D].rearrange("p (t d) -> p t d", t=T)
        v_f = arena_b[:, 0:KPAD]
        v_i = arena_b[:, KPAD:KPAD + half].bitcast(i16)
        v_b = arena_b[:, KPAD:KPAD + half].bitcast(bf16)
        x_t = xt[:, :].rearrange("p (k q) -> p k q", k=DC)
        attn = xt[:, :].rearrange("p (t d) -> p t d", t=T)
        q_f32 = q_t[:, :, :].rearrange("p h q -> p (h q)").bitcast(f32)
        attn_t = q_f32[:, 0:DC * T * P].rearrange("p (k q) -> p k q", k=DC)
        x2_t = q_f32[:, DC * T * P:2 * DC * T * P].rearrange("p (k q) -> p k q", k=DC)
        y_sb = v_q[:, :, :].rearrange("p c d -> p (c d)").bitcast(f32)[:, 0:T * D].rearrange("p (t d) -> p t d", t=T)
        wp_sb = w_qkv[:, 0, :, :]
        h_act = proj_f
        h_mul = proj_d
        h_t = proj_r
        rank_tmp = arena_b[:, 0:T * E * E].rearrange("p (t e f) -> p t e f", t=T, e=E)
        rank_eq = arena_b[:, T * E * E:2 * T * E * E].rearrange("p (t e f) -> p t e f", t=T, e=E)

        s_x, s_wq, s_wk, s_wv, s_wp, s_small = map(sem, ["x_in", "wq_in", "wk_in", "wv_in", "wp_in", "small_in"])
        s_ctx = sem("ctx_in")
        s_pad = sem("pads_zeroed")
        s_ident = sem("ident_ready")
        s_var = sem("variance_ready")
        s_std = sem("std_ready")
        s_xn = sem("normed_ready")
        s_tr = sem("transposes_done")
        s_xt = sem("transposed_copied")
        s_proj = sem("projection_done")
        s_pf = sem("projection_read")
        s_kd = sem("dequantised_ready")
        s_hi = sem("high_part_ready")
        s_rest = sem("rest_ready")
        s_mid = sem("middle_part_ready")
        s_parts = sem("low_part_ready")
        s_qb = sem("query_integers_ready")
        s_qt = [sem("query_transposed_0"), sem("query_transposed_1")]
        s_kp = [sem("key_parts_stored_0"), sem("key_parts_stored_1")]
        s_vps = sem("value_product_done")
        s_vf = sem("values_copied")
        s_vi = sem("value_integers_made")
        s_vb = sem("value_integers_ready")
        s_vq = sem("values_transposed")
        s_buf = sem("attention_pads_zeroed")
        s_kt = [sem("keys_in_0"), sem("keys_in_1")]
        s_qk = sem("scores_done")
        s_bias = sem("exp_bias_ready")
        s_exp = sem("exp_done")
        s_conv = sem("probabilities_ready")
        s_pt = [sem("probabilities_transposed_0"), sem("probabilities_transposed_1")]
        s_av = sem("head_output_done")
        s_ao = sem("head_output_copied")
        s_attn = sem("attention_normalised")
        s_otr = sem("attention_transposes_done")
        s_ot = sem("attention_transposed_copied")
        s_out = sem("out_projection_done")
        s_x1 = sem("residual_ready")
        s_gate = sem("gate_values_ready")
        s_lg = sem("logits_done")
        s_lgc = sem("logits_centred")
        s_sc = sem("score_exps_done")
        s_w = sem("routing_weights_ready")
        s_up_in = [sem("up_weights_in_0"), sem("up_weights_in_1")]
        s_dn_in = [sem("down_weights_in_0"), sem("down_weights_in_1")]
        s_h = sem("up_products_done")
        s_silu = sem("silu_done")
        s_hm = sem("hidden_ready")
        s_htr = sem("hidden_transposes_done")
        s_ht = sem("hidden_transposed_copied")
        s_y = sem("down_product_done")
        s_ya = sem("expert_added")
        s_store = sem("output_ready")
        s_done = sem("output_stored")
        s_dve = sem("dve_chain")
        s_act = sem("act_chain")
        s_pool = sem("pool_chain")
        s_sp = sem("sp_waits_passed")

        NP = T + KT

        def spread(a, shape):
            return a.unsqueeze(2).to_broadcast(shape)

        NTILE = H * T
        UN = 2 * T
        BODIES = NTILE // UN
        EB = EX // 2

        block = ctx.enter_context(nc.Block())

        @block.sync
        def _(sp):
            sp.wait_ge(s_pad, 1)
            sp.dma_start(x_sb[:, 0:T - 1, :], x[0:(T - 1) * P, :].rearrange("(t p) d -> p t d", p=P)).then_inc(s_x, 16)
            sp.dma_start(x_sb[0:TAIL, T - 1, :], x[(T - 1) * P:NTOK, :]).then_inc(s_x, 16)
            sp.dma_start(w_qkv[:, 0, :, :], wq.rearrange("(k p) n -> p k n", p=P)).then_inc(s_wq, 16)
            sp.dma_start(bias_rows[:, 0, :], bq.unsqueeze(0).to_broadcast([P, D])).then_inc(s_small, 16)
            sp.dma_start(bias_rows[:, 1, :], bkv[0:D].unsqueeze(0).to_broadcast([P, D])).then_inc(s_small, 16)
            sp.dma_start(bias_rows[:, 2, :], bp.unsqueeze(0).to_broadcast([P, D])).then_inc(s_small, 16)
            sp.dma_start(gates[:, 0:1], g_xattn.unsqueeze(0).to_broadcast([P, 1])).then_inc(s_small, 16)
            sp.dma_start(gates[:, 1:2], g_ffn.unsqueeze(0).to_broadcast([P, 1])).then_inc(s_small, 16)
            with nc.allow_non_contiguous_dma(reason="512 words"):
                sp.dma_start(bv_col[:, :], bkv[D:2 * D].rearrange("(g p) -> p g", p=P)).then_inc(s_small, 16)
            sp.dma_start(wg_sb[:, :, :], wg_t).then_inc(s_small, 16)
            sp.dma_start(w_qkv[:, 1, :, :], wkv[:, 0:D].rearrange("(k p) n -> p k n", p=P)).then_inc(s_wk, 16)
            for k in range(DC):
                sp.dma_start(ctx_sb[:, k, 0:NKEY], ctx_t[:, k, :]).then_inc(s_ctx, 16)
            sp.dma_start(w_qkv[:, 2, :, :], wkv[:, D:2 * D].rearrange("(k p) n -> p k n", p=P)).then_inc(s_wv, 16)
            for t in range(T):
                sp.wait_ge(s_qb, t + 1)
                sp.dma_start_transpose(q_t[:, :, t * P:(t + 1) * P],
                                       parts[:, t % 2].rearrange("p h g d -> p (h g d)")).then_inc(s_qt[t % 2], 16)
            for j in range(T, NP):
                sp.wait_ge(s_parts, j - T + 1)
                kt = j - T
                sp.dma_start(key_parts[kt * P:(kt + 1) * P, :],
                             parts[:, j % 2].rearrange("p h g d -> p (h g d)")).then_inc(s_kp[j % 2], 16)
            sp.wait_ge(s_kp[T % 2], 16 * ((KT + 1) // 2))
            sp.wait_ge(s_kp[(T + 1) % 2], 16 * (KT // 2))
            for g in range(NG):
                sp.wait_ge(s_vb, g + 1)
                sp.dma_start_transpose(v_q[:, :, g * P:(g + 1) * P], v_b).then_inc(s_vq, 16)
            sp.dma_start(wp_sb, wp.rearrange("(k p) n -> p k n", p=P)).then_inc(s_wp, 16)

            def wait_tile(sem_, value):
                sp.wait_ge(sem_, value)
                sp.sem_inc(s_sp, 1)

            def load_keys(head, slot):
                sp.dma_start_transpose(k_t[slot].unsqueeze(1),
                                       key_parts[:, bass.ds(head * P, P)]).then_inc(s_kt[slot], 16)

            def transpose_p(n, k):
                wait_tile(s_conv, n - 1)
                if not isinstance(n, int) or n >= 4:
                    wait_tile(s_av, n - 3)
                sp.dma_start_transpose(p_t[k % 2], p_bf[k % 2]).then_inc(s_pt[k % 2], 16)

            def tiles(i, first, last):
                for k in range(UN):
                    n = i * UN + k
                    if not first or k >= 2:
                        transpose_p(n, k)
                    if k == 1:
                        if not first:
                            wait_tile(s_qk, NS * (i * UN))
                        load_keys(i * 2 + 1, 1)
                    if k == T + 1 and not last:
                        wait_tile(s_qk, NS * (i * UN + T))
                        load_keys(i * 2 + 2, 0)

            sp.wait_ge(s_vq, 16 * NG)
            sp.wait_ge(s_buf, 2)
            load_keys(0, 0)
            tiles(0, True, False)
            with sp.Fori(1, BODIES - 1) as i:
                tiles(i, False, False)
            tiles(BODIES - 1, False, True)
            for k in range(2):
                transpose_p(NTILE + k, k)

            def load_expert(e, slot):
                sp.dma_start(arena_a[:, slot * (UPC + DNC):slot * (UPC + DNC) + UPC].unsqueeze(1),
                             w_up[bass.ds(e, 1)].rearrange("e p n -> p e n")).then_inc(s_up_in[slot], 16)
                sp.dma_start(arena_a[:, slot * (UPC + DNC) + UPC:(slot + 1) * (UPC + DNC)].unsqueeze(1),
                             w_down[bass.ds(e, 1)].rearrange("e p n -> p e n")).then_inc(s_dn_in[slot], 16)

            sp.wait_ge(s_av, NTILE)
            load_expert(0, 0)
            load_expert(1, 1)
            with sp.Fori(1, EB) as b:
                for slot in range(2):
                    sp.wait_ge(s_y, (b * 2 + slot - 1) * T)
                    load_expert(b * 2 + slot, slot)
            for t in range(T):
                rows = P if t < T - 1 else TAIL
                sp.wait_ge(s_store, t + 1)
                sp.dma_start(out[t * P:t * P + rows, :], y_sb[0:rows, t, :]).then_inc(s_done, 16)
            sp.wait_ge(s_done, 16 * T)

        @block.tensor
        def _(pe):
            mm = nc.tensor.matmul

            def transpose_tokens(src, done, ready, wait_count, copied, base):
                for t in range(T):
                    pe.wait_ge(ready, wait_count(t))
                    if t >= 2:
                        pe.wait_ge(copied, base + t - 1)
                    for k in range(DC):
                        last = nc.tensor.transpose(ps[:, t % 2, k * P:(k + 1) * P],
                                                   src[:, t, k * P:(k + 1) * P], ident[:, :])
                    last.then_inc(done, 1)

            pe.wait_ge(s_ident, 1)
            transpose_tokens(xn, s_tr, s_xn, lambda t: t + 1, s_xt, 0)
            pe.wait_ge(s_wq, 16)
            for j in range(NP):
                if j < T:
                    pe.wait_ge(s_xt, j + 1)
                if j == T:
                    pe.wait_ge(s_wk, 16)
                    pe.wait_ge(s_ctx, 16 * DC)
                if j >= 2:
                    pe.wait_ge(s_pf, j - 1)
                for k in range(DC):
                    src = x_t[:, k, j * P:(j + 1) * P] if j < T else ctx_sb[:, k, (j - T) * P:(j - T + 1) * P]
                    last = mm(ps[:, 2 + j % 2, :], src, w_qkv[:, 0 if j < T else 1, k, :],
                              start=(k == 0), stop=(k == DC - 1))
                last.then_inc(s_proj, 1)
            pe.wait_ge(s_wv, 16)
            NV = (NKEY + BANK - 1) // BANK
            for v in range(NG * NV):
                g, c = divmod(v, NV)
                w = min(BANK, NKEY - c * BANK)
                if v >= 2:
                    pe.wait_ge(s_vf, v - 1)
                for k in range(DC):
                    last = mm(ps[:, 4 + v % 2, 0:w], w_qkv[:, 2, k, g * P:(g + 1) * P],
                              ctx_sb[:, k, c * BANK:c * BANK + w], start=(k == 0), stop=(k == DC - 1))
                last.then_inc(s_vps, 1)

            def scores(i, n, k):
                slot, t = divmod(k, T)
                if t == 0:
                    pe.wait_ge(s_kt[slot], 16 * (i + 1))
                for a, w, begins, ends in PIECES:
                    if begins is not None and not (isinstance(n, int) and n == 0):
                        pe.wait_ge(s_exp, NS * (n - 1) + begins + 1)
                    last = mm(ps_flat[:, a:a + w], q_t[0:3 * HD, bass.ds(i * 2 + slot, 1), t * P:(t + 1) * P]
                              .rearrange("p h q -> p (h q)"), k_t[slot][0:3 * HD, a:a + w], start=True, stop=True)
                    if ends is not None:
                        last.then_inc(s_qk, 1)

            def weigh_values(i, n, k):
                slot, t = divmod(k, T)
                head = i * 2 + slot
                m = n - 3
                pe.wait_ge(s_pt[k % 2], 16 * (i * (UN // 2) + k // 2 + 1))
                if not isinstance(n, int) or m >= 2:
                    pe.wait_ge(s_ao, m - 1)
                for c in range(KT):
                    last = mm(ps[:, 6 + k % 2, 0:HD], p_t[k % 2][:, c, :], v_q[:, c, bass.ds(head * HD, HD)],
                              start=(c == 0), stop=(c == KT - 1))
                last.then_inc(s_av, 1)

            def tiles(i, first):
                for k in range(UN):
                    n = i * UN + k
                    scores(i, n, k)
                    if k >= 3:
                        weigh_values(i, n, k - 3)
                    elif not first:
                        weigh_values(i - 1, n, k - 3 + UN)

            pe.wait_ge(s_qt[0], 16 * ((T + 1) // 2))
            pe.wait_ge(s_qt[1], 16 * (T // 2))
            pe.wait_ge(s_vq, 16 * NG)
            tiles(0, True)
            with pe.Fori(1, BODIES) as i:
                tiles(i, False)
            for k in range(3):
                weigh_values(BODIES - 1, NTILE + k, UN - 3 + k)

            transpose_tokens(attn, s_otr, s_attn, lambda t: 1, s_ot, 0)
            pe.wait_ge(s_wp, 16)
            for t in range(T):
                pe.wait_ge(s_ot, t + 1)
                if t >= 2:
                    pe.wait_ge(s_x1, t - 1)
                for k in range(DC):
                    last = mm(ps[:, 2 + t % 2, :], attn_t[:, k, t * P:(t + 1) * P], wp_sb[:, k, :],
                              start=(k == 0), stop=(k == DC - 1))
                last.then_inc(s_out, 1)
            transpose_tokens(xn, s_tr, s_xn, lambda t: T + t + 1, s_xt, T)
            pe.wait_ge(s_xt, 2 * T)
            for t in range(T):
                for k in range(DC):
                    last = mm(ps[:, 4, t * E:(t + 1) * E], x2_t[:, k, t * P:(t + 1) * P], wg_sb[:, k, :],
                              start=(k == 0), stop=(k == DC - 1))
            last.then_inc(s_lg, 1)

            def up(b, slot, t, u):
                for w in range(2):
                    for k in range(DC):
                        last = mm(ps[:, 2 * (t % 2) + w, 0:INTER], x2_t[:, k, t * P:(t + 1) * P],
                                  up_sb[slot][:, w, k, :], start=(k == 0), stop=(k == DC - 1))
                last.then_inc(s_h, 1)

            def down(b, slot, t, u):
                pe.wait_ge(s_hm, u + 1)
                for c in range(IC):
                    last = nc.tensor.transpose(ps[0:IW[c], 4, c * P:(c + 1) * P],
                                               h_mul[:, u_par(t, slot), c * P:c * P + IW[c]], ident[:, :])
                last.then_inc(s_htr, 1)
                pe.wait_ge(s_ht, u + 1)
                for c in range(IC):
                    last = mm(ps[:, 6 + u_par(t, slot), :], h_t[0:IW[c], u_par(t, slot), c * P:(c + 1) * P],
                              down_sb[slot][0:IW[c], c, :], start=(c == 0), stop=(c == IC - 1))
                last.then_inc(s_y, 1)

            def u_par(t, slot):
                return (slot * T + t) % 2

            def experts(b, first):
                for slot in range(2):
                    pe.wait_ge(s_up_in[slot], 16 * (b + 1))
                    pe.wait_ge(s_dn_in[slot], 16 * (b + 1))
                    for t in range(T):
                        u = (b * 2 + slot) * T + t
                        if not (first and slot == 0 and t == 0):
                            pe.wait_ge(s_hm, u)
                        up(b, slot, t, u)
                        down(b, slot, t, u)

            pe.wait_ge(s_lgc, 1)
            experts(0, True)
            with pe.Fori(1, EB) as b:
                experts(b, False)

        @block.scalar
        def _(act):
            chain = [0]

            def link(ins):
                chain[0] += 1
                ins.then_inc(s_act, 1)
                act.wait_ge(s_act, chain[0])

            act.wait_ge(s_var, 1)
            nc.scalar.activation(std[:, :], std[:, :], ACT.Sqrt).then_inc(s_std, 1)

            def copy_transposed(done, count, copied, dst, scale=None):
                for t in range(T):
                    act.wait_ge(done, count + t + 1)
                    src = ps[:, t % 2, :].rearrange("p (k q) -> p k q", k=DC)
                    if scale is None:
                        last = nc.scalar.copy(dst[:, :, t * P:(t + 1) * P], src)
                    else:
                        for k in range(DC):
                            last = nc.scalar.activation(dst[:, k, t * P:(t + 1) * P], src[:, k, :], ACT.Copy,
                                                        scale=scale[:, k:k + 1])
                    last.then_inc(copied, 1)

            copy_transposed(s_tr, 0, s_xt, x_t)
            for kt in range(KT):
                j = T + kt
                act.wait_ge(s_kd, kt + 1)
                if kt < 2:
                    act.wait_ge(s_qt[j % 2], 16 * ((T + 1 - j % 2) // 2))
                else:
                    act.wait_ge(s_kp[j % 2], 16 * (kt // 2))
                nc.scalar.copy(parts[:, j % 2, :, 0, :], proj_d[:, j % 2, :].rearrange("p (h d) -> p h d", h=H)
                               ).then_inc(s_hi, 1)
                act.wait_ge(s_rest, kt + 1)
                nc.scalar.copy(parts[:, j % 2, :, 1, :], proj_r[:, j % 2, :].rearrange("p (h d) -> p h d", h=H)
                               ).then_inc(s_mid, 1)
            act.wait_ge(s_small, 16 * 7)
            NV = (NKEY + BANK - 1) // BANK
            for v in range(NG * NV):
                g, c = divmod(v, NV)
                w = min(BANK, NKEY - c * BANK)
                act.wait_ge(s_vps, v + 1)
                if c == 0 and g:
                    act.wait_ge(s_vi, g)
                nc.scalar.activation(v_f[:, c * BANK:c * BANK + w], ps[:, 4 + v % 2, 0:w], ACT.Identity,
                                     bias=bv_col[:, g:g + 1]).then_inc(s_vf, 1)
            act.wait_ge(s_small, 16 * 7)
            nc.scalar.activation(gates[:, :], gates[:, :], ACT.Tanh).then_inc(s_gate, 1)

            def exps(i, n, k):
                slot, t = divmod(k, T)
                head = i * 2 + slot
                act.wait_ge(s_bias, n + 1)
                if not isinstance(n, int) or n >= 2:
                    act.wait_ge(s_conv, n - 1)
                for s, (a, w) in enumerate(SPANS):
                    nc.scalar.activation(p_int[k % 2][:, a:a + w], ps_flat[:, a:a + w], ACT.Exp,
                                         bias=exp_bias[:, k % 2:k % 2 + 1],
                                         scale=q_step[:, bass.ds(head, 1), t],
                                         accum_out=exp_sums[:, bass.ds(head, 1), t, s]).then_inc(s_exp, 1)

            def keep_output(i, n, k):
                slot, t = divmod(k, T)
                act.wait_ge(s_av, n - 3)
                nc.scalar.copy(attn[:, t, bass.ds((i * 2 + slot) * HD, HD)], ps[:, 6 + k % 2, 0:HD]).then_inc(s_ao, 1)

            def tiles(i, first):
                for k in range(UN):
                    n = i * UN + k
                    exps(i, n, k)
                    if k >= 4:
                        keep_output(i, n, k - 4)
                    elif not first:
                        keep_output(i - 1, n, k - 4 + UN)

            act.wait_ge(s_buf, 2)
            tiles(0, True)
            with act.Fori(1, BODIES) as i:
                tiles(i, False)
            for k in range(4):
                keep_output(BODIES - 1, NTILE + k, UN - 4 + k)

            copy_transposed(s_otr, 0, s_ot, attn_t, v_step)
            act.wait_ge(s_var, 2)
            nc.scalar.activation(std[:, :], std[:, :], ACT.Sqrt).then_inc(s_std, 1)
            copy_transposed(s_tr, T, s_xt, x2_t)
            act.wait_ge(s_lgc, 1)
            nc.scalar.activation(score[:, :, :], logit[:, :, :], ACT.Exp).then_inc(s_sc, 1)

            def hidden(u, k):
                act.wait_ge(s_h, u + 1)
                nc.scalar.activation(h_act[:, k % 2, 0:INTER], ps[:, 2 * (k % T % 2), 0:INTER], ACT.Silu
                                     ).then_inc(s_silu, 1)
                act.wait_ge(s_htr, u + 1)
                for c in range(IC):
                    last = nc.scalar.copy(h_t[0:IW[c], k % 2, c * P:(c + 1) * P], ps[0:IW[c], 4, c * P:(c + 1) * P])
                last.then_inc(s_ht, 1)

            with act.Fori(0, EB) as b:
                for k in range(2 * T):
                    hidden(b * 2 * T + k, k)

        @block.vector
        def _(dve):
            v = nc.vector
            chain = [0]

            def link(ins):
                chain[0] += 1
                ins.then_inc(s_dve, 1)
                dve.wait_ge(s_dve, chain[0])

            def layer_norm(n):
                for t in range(T):
                    last = v.bn_stats(stats[:, t, :], x_sb[:, t, :])
                link(last)
                for t in range(T):
                    last = v.bn_aggr(mean_var[:, t, :], stats[:, t, :])
                link(last)
                v.tensor_scalar_add(std[:, :], mean_var[:, :, 1], LN_EPS).then_inc(s_var, 1)
                dve.wait_ge(s_std, n)
                link(v.reciprocal(std[:, :], std[:, :]))
                for t in range(T):
                    v.tensor_scalar(xn[:, t, :], x_sb[:, t, :], mean_var[:, t, 0:1], std[:, t:t + 1],
                                    ALU.subtract, ALU.mult).then_inc(s_xn, 1)

            dve.wait_ge(s_x, 32)
            layer_norm(1)

            dve.wait_ge(s_small, 16 * 7)
            for j in range(NP):
                b = j % 2
                kt = j - T
                pf = proj_f[:, b, :]
                heads = lambda a: a.rearrange("p (h d) -> p h d", h=H)
                dve.wait_ge(s_proj, j + 1)
                chain[0] += 1
                ins = v.tensor_tensor(pf, ps[:, 2 + b, :], bias_rows[:, 0 if j < T else 1, :], ALU.add)
                ins.then_inc(s_pf, 1)
                chain[0] -= 1
                dve.wait_ge(s_pf, j + 1)
                if j < T:
                    link(v.tensor_scalar(pf, pf, QSCALE, None, ALU.mult))
                link(v.tensor_reduce(amax[:, b, :], heads(pf), AX.X, ALU.max, apply_absolute_value=True))
                st = q_step[:, :, j] if j < T else step[:, b, :]
                link(v.tensor_scalar(st, amax[:, b, :], 1.0 / 127.0, 1e-8, ALU.mult, ALU.max))
                if j < T:
                    v.tensor_scalar(neg_q_step[:, :, j], st, -1.0, None, ALU.mult)
                link(v.reciprocal(inv_step[:, b, :], st))
                link(v.tensor_tensor(heads(proj_i[:, b, :]), heads(pf), spread(inv_step[:, b, :], [P, H, HD]), ALU.mult))
                if j < T:
                    if j >= 2:
                        dve.wait_ge(s_qt[b], 16 * (j // 2))
                    v.tensor_copy(parts[:, b].rearrange("p h g d -> p g h d"),
                                  proj_i[:, b, :].rearrange("p (h d) -> p h d", h=H).unsqueeze(1)
                                  .to_broadcast([P, HG, H, HD])).then_inc(s_qb, 1)
                else:
                    if kt >= 2:
                        dve.wait_ge(s_rest, kt - 1)
                        dve.wait_ge(s_hi, kt - 1)
                    v.tensor_tensor(heads(proj_d[:, b, :]), heads(proj_i[:, b, :]), spread(step[:, b, :], [P, H, HD]),
                                    ALU.mult).then_inc(s_kd, 1)

            NV = (NKEY + BANK - 1) // BANK
            for g in range(NG):
                dve.wait_ge(s_vf, NV * (g + 1))
                link(v.tensor_reduce(v_amax[:, g:g + 1], v_f[:, 0:NKEY], AX.X, ALU.max, apply_absolute_value=True))
                link(v.tensor_scalar(v_step[:, g:g + 1], v_amax[:, g:g + 1], 1.0 / 127.0, 1e-8, ALU.mult, ALU.max))
                link(v.reciprocal(v_inv[:, g:g + 1], v_step[:, g:g + 1]))
                if g:
                    dve.wait_ge(s_vq, 16 * g)
                else:
                    link(v.memset(v_i[:, NKEY:KPAD], 0))
                v.tensor_scalar(v_i[:, 0:NKEY], v_f[:, 0:NKEY], v_inv[:, g:g + 1], None, ALU.mult).then_inc(s_vi, 1)
                dve.wait_ge(s_vi, g + 1)
                v.tensor_copy(v_b[:, 0:NKEY], v_i[:, 0:NKEY]).then_inc(s_vb, 1)

            dve.wait_ge(s_vps, NG * NV)
            for i in range(2):
                v.memset(p_int[i][:, NKEY:KPAD], 0).then_inc(s_buf, 1)
            dve.wait_ge(s_buf, 2)

            def to_bf16(i, n, k):
                dve.wait_ge(s_exp, NS * (n - 1))
                if not isinstance(n, int) or n >= 4:
                    dve.wait_ge(s_pt[k % 2], 16 * (i * (UN // 2) + k // 2))
                v.tensor_copy(p_bf[k % 2], p_int[k % 2]).then_inc(s_conv, 1)

            LINKS = NS + 1

            def maximum(i, n, k, base):
                slot, t = divmod(k, T)
                for s, (a, w) in enumerate(SPANS):
                    dve.wait_ge(s_qk, NS * n + s + 1)
                    v.tensor_reduce(span_max[:, k % 2, s:s + 1], ps_flat[:, a:a + w], AX.X, ALU.max).then_inc(s_dve, 1)
                dve.wait_ge(s_dve, base + LINKS * n + NS)
                v.tensor_reduce(row_max[:, k % 2:k % 2 + 1], span_max[:, k % 2, :], AX.X, ALU.max).then_inc(s_dve, 1)
                dve.wait_ge(s_dve, base + LINKS * n + NS + 1)
                v.tensor_scalar(exp_bias[:, k % 2:k % 2 + 1], row_max[:, k % 2:k % 2 + 1],
                                neg_q_step[:, bass.ds(i * 2 + slot, 1), t], LOG255, ALU.mult, ALU.add
                                ).then_inc(s_bias, 1)

            def tiles(i, first, base):
                for k in range(UN):
                    n = i * UN + k
                    if k >= 2:
                        to_bf16(i, n, k - 2)
                    elif not first:
                        to_bf16(i - 1, n, k - 2 + UN)
                    maximum(i, n, k, base)

            base = chain[0]
            tiles(0, True, base)
            with dve.Fori(1, BODIES) as i:
                tiles(i, False, base)
            chain[0] = base + LINKS * NTILE
            for k in range(2):
                to_bf16(BODIES - 1, NTILE + k, UN - 2 + k)

            dve.wait_ge(s_exp, NS * NTILE)
            link(v.tensor_reduce(inv_sum[:, :, :], exp_sums[:, :, :, :], AX.X, ALU.add))
            link(v.reciprocal(inv_sum[:, :, :], inv_sum[:, :, :]))
            link(v.tensor_scalar(inv_sum[:, :, :], inv_sum[:, :, :], 1e-8, None, ALU.max))
            dve.wait_ge(s_ao, NTILE)
            for t in range(T):
                a = attn[:, t, :].rearrange("p (h d) -> p h d", h=H)
                last = v.tensor_tensor(a, a, spread(inv_sum[:, :, t], [P, H, HD]), ALU.mult)
            last.then_inc(s_attn, 1)

            dve.wait_ge(s_gate, 1)
            for t in range(T):
                dve.wait_ge(s_out, t + 1)
                link(v.tensor_tensor(proj_f[:, 0, :], ps[:, 2 + t % 2, :], bias_rows[:, 2, :], ALU.add))
                v.scalar_tensor_tensor(x_sb[:, t, :], proj_f[:, 0, :], gates[:, 0:1], x_sb[:, t, :],
                                       ALU.mult, ALU.add).then_inc(s_x1, 1)
                dve.wait_ge(s_x1, t + 1)
            layer_norm(2)

            dve.wait_ge(s_lg, 1)
            link(v.tensor_copy(logit[:, :, :], ps[:, 4, 0:T * E].rearrange("p (t e) -> p t e", t=T)))
            link(v.tensor_reduce(tok[:, :], logit[:, :, :], AX.X, ALU.max))
            v.tensor_tensor(logit[:, :, :], logit[:, :, :], spread(tok[:, :], [P, T, E]), ALU.subtract).then_inc(s_lgc, 1)
            dve.wait_ge(s_sc, 1)
            link(v.tensor_reduce(tok[:, :], score[:, :, :], AX.X, ALU.add))
            link(v.reciprocal(tok[:, :], tok[:, :]))
            link(v.tensor_tensor(score[:, :, :], score[:, :, :], spread(tok[:, :], [P, T, E]), ALU.mult))
            link(v.tensor_reduce(grp[:, :, :], score[:, :, :].rearrange("p t (g e) -> p t g e", g=EG), AX.X, ALU.max))

            def ranks(dst, a, n, mask, tmp, eq):
                shape = [P, T, n, n]
                other, own = a.unsqueeze(2).to_broadcast(shape), a.unsqueeze(3).to_broadcast(shape)
                v.tensor_tensor(tmp, other, own, ALU.is_gt)
                link(v.tensor_tensor(eq, other, own, ALU.is_equal))
                link(v.tensor_tensor(eq, eq, mask.unsqueeze(1).to_broadcast(shape), ALU.mult))
                link(v.tensor_tensor(tmp, tmp, eq, ALU.add))
                link(v.tensor_reduce(dst, tmp, AX.X, ALU.add))

            dve.wait_ge(s_tr, 2 * T)
            small = lambda a: arena_b[:, a:a + T * EG * EG].rearrange("p (t e f) -> p t e f", t=T, e=EG)
            dve.wait_ge(s_pool, 4)
            ranks(grp_rank[:, :, :], grp[:, :, :], EG, before_g[:, :, :], small(0), small(T * EG * EG))
            link(v.tensor_scalar(grp[:, :, :], grp_rank[:, :, :], TOPG - 0.5, None, ALU.is_lt))
            link(v.tensor_scalar(grp_rank[:, :, :], grp[:, :, :], -1.0, None, ALU.add))
            by_group = lambda a: a.rearrange("p t (g e) -> p t g e", g=EG)
            gs = [P, T, EG, E // EG]
            link(v.tensor_tensor(by_group(logit[:, :, :]), by_group(score[:, :, :]),
                                 grp[:, :, :].unsqueeze(3).to_broadcast(gs), ALU.mult))
            link(v.tensor_tensor(by_group(logit[:, :, :]), by_group(logit[:, :, :]),
                                 grp_rank[:, :, :].unsqueeze(3).to_broadcast(gs), ALU.add))
            ranks(rank[:, :, :], logit[:, :, :], E, before[:, :, :], rank_tmp, rank_eq)
            link(v.tensor_scalar(rank[:, :, :], rank[:, :, :], TOPK - 0.5, None, ALU.is_lt))
            v.memset(weight[:, :, E:EX], 1.0)
            link(v.tensor_tensor(weight[:, :, 0:E], rank[:, :, :], score[:, :, :], ALU.mult))
            v.memset(y_sb[:, :, :], 0.0).then_inc(s_ya, 1)

            def expert_tile(b, k):
                slot, t = divmod(k, T)
                u = b * 2 * T + k
                dve.wait_ge(s_silu, u + 1)
                v.tensor_tensor(h_mul[:, k % 2, 0:INTER], ps[:, 2 * (t % 2) + 1, 0:INTER], h_act[:, k % 2, 0:INTER],
                                ALU.mult).then_inc(s_hm, 1)
                dve.wait_ge(s_y, u + 1)
                dve.wait_ge(s_ya, u + 1)
                v.scalar_tensor_tensor(y_sb[:, t, :], ps[:, 6 + k % 2, :], weight[:, t, bass.ds(b * 2 + slot, 1)],
                                       y_sb[:, t, :], ALU.mult, ALU.add).then_inc(s_ya, 1)

            with dve.Fori(0, EB) as b:
                for k in range(2 * T):
                    expert_tile(b, k)

            dve.wait_ge(s_ya, EX * T + 1)
            for t in range(T):
                v.scalar_tensor_tensor(y_sb[:, t, :], y_sb[:, t, :], gates[:, 1:2], x_sb[:, t, :],
                                       ALU.mult, ALU.add).then_inc(s_store, 1)

        @block.gpsimd
        def _(pool):
            p = nc.gpsimd
            p.memset(x_sb[:, T - 1, :], 0.0).then_inc(s_pad, 1)
            p.memset(ctx_sb[:, :, NKEY:KPAD], 0.0).then_inc(s_pool, 1)
            p.memset(ident[:, :], 0.0).then_inc(s_pool, 1)
            pool.wait_ge(s_pool, 2)
            p.affine_select(out=ident[:, :], in_=ident[:, :], compare_op=ALU.not_equal, fill=1.0, base=0,
                            pattern=[[-1, P]], channel_multiplier=1).then_inc(s_ident, 1)
            p.memset(before[:, :, :], 1.0).then_inc(s_pool, 1)
            pool.wait_ge(s_pool, 3)
            p.affine_select(out=before[:, :, :], in_=before[:, :, :], compare_op=ALU.is_gt, fill=0.0, base=0,
                            pattern=[[1, E], [-1, E]], channel_multiplier=0).then_inc(s_pool, 1)
            p.memset(before_g[:, :, :], 1.0).then_inc(s_ident, 1)
            pool.wait_ge(s_ident, 2)
            p.affine_select(out=before_g[:, :, :], in_=before_g[:, :, :], compare_op=ALU.is_gt, fill=0.0, base=0,
                            pattern=[[1, EG], [-1, EG]], channel_multiplier=0).then_inc(s_pool, 1)
            for kt in range(KT):
                j = T + kt
                b = j % 2
                heads = lambda a: a.rearrange("p (h d) -> p h d", h=H)
                pool.wait_ge(s_kd, kt + 1)
                pool.wait_ge(s_hi, kt + 1)
                p.tensor_tensor(heads(proj_r[:, b, :]), heads(proj_d[:, b, :]), parts[:, b, :, 0, :],
                                ALU.subtract).then_inc(s_rest, 1)
                pool.wait_ge(s_rest, kt + 1)
                pool.wait_ge(s_mid, kt + 1)
                p.tensor_tensor(parts[:, b, :, 2, :], heads(proj_r[:, b, :]), parts[:, b, :, 1, :],
                                ALU.subtract).then_inc(s_parts, 1)


def kernel(**inputs):
    import numpy as _np
    import concourse.bacc as _bacc
    from concourse import mybir as _mybir
    from concourse.bass_utils import run_bass_kernel_spmd as _run

    P = 128
    a = {k: _np.asarray(v) for k, v in inputs.items()}
    x, ctx = a["x"], a["ctx_2048"]
    D = x.shape[-1]
    DC = D // P
    w1, w3, w2 = a["L0_ffn_W1"], a["L0_ffn_W3"], a["L0_ffn_W2"]
    E, I = w1.shape[:2]
    s1 = a["L0_ffn_Ws1"].reshape(-1, I, D)
    s3 = a["L0_ffn_Ws3"].reshape(-1, I, D)
    s2 = a["L0_ffn_Ws2"].reshape(D, -1, I).transpose(1, 0, 2)
    IC = (I + P - 1) // P

    def up(w):
        return w.reshape(-1, I, DC, P).transpose(0, 3, 2, 1)

    def down(w):
        full = _np.zeros((w.shape[0], IC * P, D), w.dtype)
        full[:, :I] = w.transpose(0, 2, 1)
        return full.reshape(-1, IC, P, D).transpose(0, 2, 1, 3)

    ups = _np.stack([_np.concatenate([up(w1), up(s1)]), _np.concatenate([up(w3), up(s3)])], axis=2)
    downs = _np.concatenate([down(w2), down(s2)])
    laid = {
        "x": x.reshape(-1, D),
        "ctx_t": ctx.reshape(-1, DC, P).transpose(2, 1, 0),
        "g_xattn": a["g_xattn"],
        "g_ffn": a["g_ffn"],
        "wq": a["L0_xattn_Wq"],
        "bq": a["L0_xattn_bq"],
        "wkv": a["L0_xattn_Wkv"],
        "bkv": a["L0_xattn_bkv"],
        "wp": a["L0_xattn_Wp"],
        "bp": a["L0_xattn_bp"],
        "wg_t": a["L0_ffn_Wg"].reshape(E, DC, P).transpose(2, 1, 0),
        "w_up": ups.reshape(ups.shape[0], P, -1),
        "w_down": downs.reshape(downs.shape[0], P, -1),
    }
    laid = {k: _np.ascontiguousarray(v) for k, v in laid.items()}
    nc = _bacc.Bacc("TRN2", target_bir_lowering=False, num_devices=1)
    args = [nc.dram_tensor(f"in_{k}", v.shape, _mybir.dt.from_np(v.dtype), kind="ExternalInput").ap()
            for k, v in laid.items()]
    args.append(nc.dram_tensor("out_0", laid["x"].shape, _mybir.dt.float32, kind="ExternalOutput").ap())
    gated_xattn_moe_kernel(nc, *args)
    r = _run(nc, [{f"in_{k}": v for k, v in laid.items()}], core_ids=[0])
    return r.results[0]["out_0"].reshape(x.shape)
```

```python
import math
from contextlib import ExitStack

import concourse.bass as bass
from concourse import mybir


def gated_xattn_moe_kernel(
    nc: bass.Bass,
    x: bass.AP,
    ctx_t: bass.AP,
    g_xattn: bass.AP,
    g_ffn: bass.AP,
    wq: bass.AP,
    bq: bass.AP,
    wkv: bass.AP,
    bkv: bass.AP,
    wp: bass.AP,
    bp: bass.AP,
    wg_t: bass.AP,
    w_up: bass.AP,
    w_down: bass.AP,
    out: bass.AP,
):
    f32, bf16, i16 = mybir.dt.float32, mybir.dt.bfloat16, mybir.dt.int16
    ALU, ACT, AX = mybir.AluOpType, mybir.ActivationFunctionType, mybir.AxisListType

    P = 128
    NTOK, D = x.shape
    DC = D // P
    NKEY = ctx_t.shape[2]
    H, HD = 16, 32
    HG = P // HD
    NG = H // HG
    T = (NTOK + P - 1) // P
    TAIL = NTOK - (T - 1) * P
    KT = (NKEY + P - 1) // P
    KPAD = KT * P
    E = wg_t.shape[2]
    EX = w_up.shape[0]
    INTER = w_up.shape[2] // (2 * DC)
    IC = w_down.shape[2] // D
    IW = [min(P, INTER - P * c) for c in range(IC)]
    EG, TOPG, TOPK = 4, 2, 4
    SHARED = EX - E
    MAXT = (NTOK * TOPK - E) // P + E + 1
    MINT = NTOK * TOPK // P
    LN_EPS = 1e-5
    QSCALE = 1.0 / math.sqrt(HD)
    LOG255 = math.log(255.0)
    BANK = 512

    BANK_SPANS = lambda banks: [(a * BANK, min(b * BANK, NKEY) - a * BANK) for a, b in zip(banks, banks[1:])]
    MAX_SPANS, MAX_BANK = BANK_SPANS([0, 2, 3, 5, 6]), [0, 2]
    EXP_SPANS, EXP_BANK = BANK_SPANS([0, 2, 4, 6]), [3, 5]
    NM, NE, OUT_BANK = len(MAX_SPANS), len(EXP_SPANS), 7

    ctx = ExitStack()
    with ctx:
        def sb(name, shape, dt):
            return ctx.enter_context(nc.sbuf_tensor(name, shape, dt))

        def sem(name):
            return ctx.enter_context(nc.semaphore(name))

        key_parts = nc.dram_tensor("key_parts", [KPAD, H * P], bf16, kind="Internal").ap()

        expert_in = nc.dram_tensor("expert_in", [(MAXT + 1) * P, D], f32, kind="Internal").ap()
        expert_out = nc.dram_tensor("expert_out", [(MAXT + 1) * P, D], f32, kind="Internal").ap()

        arena_a = sb("arena_a", [P, DC * KPAD], f32)
        arena_b = sb("arena_b", [P, 4608], f32)
        x_sb = sb("x_sb", [P, T, D], f32)
        w_qkv = sb("w_qkv", [P, 3, DC, D], f32)
        bias_rows = sb("bias_rows", [P, 3, D], f32)
        bv_col = sb("bv_col", [P, NG], f32)
        xt = sb("xt", [P, T * D], f32)
        q_t = sb("q_t", [P, H, T * P], bf16)
        v_q = sb("v_q", [P, KT, D], bf16)
        proj_f = sb("proj_f", [P, 2, D], f32)
        proj_i = sb("proj_i", [P, 2, D], i16)
        proj_d = sb("proj_d", [P, 2, D], f32)
        proj_r = sb("proj_r", [P, 2, D], f32)
        parts = sb("parts", [P, 2, H, HG, HD], bf16)
        ident = sb("ident", [P, P], f32)
        gates = sb("gates", [P, 2], f32)
        wg_sb = sb("wg_sb", [P, DC, E], f32)
        stats = sb("stats", [P, T, 6], f32)
        mean_var = sb("mean_var", [P, T, 2], f32)
        std = sb("std", [P, T], f32)
        amax = sb("amax", [P, 2, H], f32)
        step = sb("step", [P, 2, H], f32)
        inv_step = sb("inv_step", [P, 2, H], f32)
        v_amax = sb("v_amax", [P, NG], f32)
        v_step = sb("v_step", [P, NG], f32)
        v_inv = sb("v_inv", [P, NG], f32)
        q_step = sb("q_step", [P, H, T], f32)
        neg_q_step = sb("neg_q_step", [P, H, T], f32)
        span_max = sb("span_max", [P, 2, NM], f32)
        row_max = sb("row_max", [P, 2], f32)
        exp_bias = sb("exp_bias", [P, 2], f32)
        exp_sums = sb("exp_sums", [P, H, T, NE], f32)
        inv_sum = sb("inv_sum", [P, H, T], f32)
        logit = sb("logit", [P, T, E], f32)
        score = sb("score", [P, T, E], f32)
        tok = sb("tok", [P, T], f32)
        grp = sb("grp", [P, T, EG], f32)
        grp_rank = sb("grp_rank", [P, T, EG], f32)
        rank = sb("rank", [P, T, E], f32)
        sel = sb("sel", [P, T, E], f32)
        sel_before = sb("sel_before", [P, T, E], f32)
        sel_total = sb("sel_total", [P, E], f32)
        slot_of = sb("slot_of", [P, T, E], f32)
        slot_j = sb("slot_j", [P, TOPK, T], f32)
        slot_i = sb("slot_i", [P, TOPK, T], mybir.dt.int32)
        weight_j = sb("weight_j", [P, TOPK, T], f32)
        valid = sb("valid", [P, 1], f32)
        count = sb("count", [P, E], f32)
        thresholds = sb("thresholds", [P, T - 1], f32)
        tiles_of = sb("tiles_of", [P, E], f32)
        first_tile = sb("first_tile", [P, E], f32)
        end_tile = sb("end_tile", [P, E], f32)
        tile_no = sb("tile_no", [P, MAXT], f32)
        tile_expert = sb("tile_expert", [P, MAXT], f32)
        tile_tmp = sb("tile_tmp", [P, MAXT], f32)
        n_pairs = sb("n_pairs", [P, 2], mybir.dt.int32)
        weight_col = sb("weight_col", [P, MAXT], mybir.dt.int32)
        weight_need = sb("weight_need", [P, MAXT], mybir.dt.int32)
        end_step = sb("end_step", [P, E], mybir.dt.int32)
        iota_i = sb("iota_i", [P, MAXT], mybir.dt.int32)
        upper = sb("upper", [P, P], f32)
        ones = sb("ones", [P, P], f32)
        before = sb("before", [P, E, E], f32)
        before_g = sb("before_g", [P, EG, EG], f32)

        ps = ctx.enter_context(nc.psum_tensor("ps", [P, 8, BANK], f32))
        ps_flat = ps[:, :, :].rearrange("p b n -> p (b n)")

        ctx_sb = arena_a[:, :].rearrange("p (k n) -> p k n", k=DC)

        def bf_view(a, cols):
            return arena_a[:, a:a + cols // 2].bitcast(bf16)

        half = KPAD // 2
        k_t = [bf_view(half * i, KPAD) for i in range(2)]
        p_int = [arena_a[:, half * (2 + i):half * (3 + i)].bitcast(i16) for i in range(2)]
        p_bf = [bf_view(half * (4 + i), KPAD) for i in range(2)]
        p_t = [bf_view(half * (6 + i), KPAD).rearrange("p (c q) -> p c q", q=P) for i in range(2)]
        UPC, DNC = 2 * DC * INTER, IC * D
        SLOT = UPC + DNC
        x_rows = xt[:, 0:2 * D].rearrange("p (b d) -> p b d", b=2)
        xe_t = xt[:, 2 * D:4 * D].rearrange("p (b k q) -> p b k q", b=2, k=DC)
        y_rows = xt[:, 4 * D:6 * D].rearrange("p (b d) -> p b d", b=2)
        xn = arena_b[:, 0:T * D].rearrange("p (t d) -> p t d", t=T)
        v_f = arena_b[:, 0:KPAD]
        v_i = arena_b[:, KPAD:KPAD + half].bitcast(i16)
        v_b = arena_b[:, KPAD:KPAD + half].bitcast(bf16)
        x_t = xt[:, :].rearrange("p (k q) -> p k q", k=DC)
        attn = xt[:, :].rearrange("p (t d) -> p t d", t=T)
        q_f32 = q_t[:, :, :].rearrange("p h q -> p (h q)").bitcast(f32)
        attn_t = q_f32[:, 0:DC * T * P].rearrange("p (k q) -> p k q", k=DC)
        x2_t = q_f32[:, DC * T * P:2 * DC * T * P].rearrange("p (k q) -> p k q", k=DC)
        y_sb = v_q[:, :, :].rearrange("p c d -> p (c d)").bitcast(f32)[:, 0:T * D].rearrange("p (t d) -> p t d", t=T)
        wp_sb = w_qkv[:, 0, :, :]
        h_act = proj_f
        h_mul = proj_d
        h_t = proj_r
        v_q32 = v_q[:, :, :].rearrange("p c d -> p (c d)").bitcast(f32)
        rank_tmp = arena_a[:, 2 * SLOT:2 * SLOT + T * E * E].rearrange("p (t e f) -> p t e f", t=T, e=E)
        rank_eq = v_q32[:, T * D:T * D + T * E * E].rearrange("p (t e f) -> p t e f", t=T, e=E)
        part_words = parts[:, :, :, :, :].rearrange("p b h g d -> p (b h g d)").bitcast(f32)
        past = part_words[:, 0:MAXT * E].rearrange("p (s e) -> p s e", e=E)
        prefix = part_words[:, MAXT * E:(MAXT + E) * E].rearrange("p (e f) -> p e f", f=E)
        over = part_words[:, (MAXT + E) * E:(MAXT + E + T - 1) * E].rearrange("p (e t) -> p e t", e=E)
        pick = part_words[:, (MAXT + E + T - 1) * E:(MAXT + E + 2 * T - 1) * E].rearrange("p (t e) -> p t e", e=E)
        NGATHER = 8
        gathered = arena_b[:, 0:NGATHER * D].rearrange("p (b d) -> p b d", b=NGATHER)

        s_x, s_wq, s_wk, s_wv, s_wp, s_small = map(sem, ["x_in", "wq_in", "wk_in", "wv_in", "wp_in", "small_in"])
        s_ctx = sem("ctx_in")
        s_pad = sem("pads_zeroed")
        s_ident = sem("ident_ready")
        s_var = sem("variance_ready")
        s_std = sem("std_ready")
        s_xn = sem("normed_ready")
        s_tr = sem("transposes_done")
        s_xt = sem("transposed_copied")
        s_proj = sem("projection_done")
        s_pf = sem("projection_read")
        s_kd = sem("dequantised_ready")
        s_hi = sem("high_part_ready")
        s_rest = sem("rest_ready")
        s_mid = sem("middle_part_ready")
        s_parts = sem("low_part_ready")
        s_qi = sem("query_integers_ready")
        s_qt = [sem("query_transposed_0"), sem("query_transposed_1")]
        s_kp = [sem("key_parts_stored_0"), sem("key_parts_stored_1")]
        s_vps = sem("value_product_done")
        s_vf = sem("values_copied")
        s_vi = sem("value_integers_made")
        s_vb = sem("value_integers_ready")
        s_vq = sem("values_transposed")
        s_buf = sem("attention_pads_zeroed")
        s_kt = [sem("keys_in_0"), sem("keys_in_1")]
        s_qa = sem("scores_for_max_done")
        s_qb = sem("scores_for_exp_done")
        s_max = sem("span_maximum_done")
        s_bias = sem("exp_bias_ready")
        s_exp = sem("exp_done")
        s_conv = sem("probabilities_ready")
        s_pt = [sem("probabilities_transposed_0"), sem("probabilities_transposed_1")]
        s_av = sem("head_output_done")
        s_ao = sem("head_output_copied")
        s_attn = sem("attention_normalised")
        s_otr = sem("attention_transposes_done")
        s_ot = sem("attention_transposed_copied")
        s_out = sem("out_projection_done")
        s_x1 = sem("residual_ready")
        s_gate = sem("gate_values_ready")
        s_lg = sem("logits_done")
        s_lgc = sem("logits_centred")
        s_sc = sem("score_exps_done")
        s_sel = sem("selection_ready")
        s_pos = sem("positions_done")
        s_slots = sem("slots_ready")
        s_zero = sem("zeros_ready")
        s_xz = sem("expert_in_zeroed")
        s_scat = [sem(f"tokens_scattered_{j}") for j in range(TOPK)]
        s_win = [sem("weights_in_0"), sem("weights_in_1")]
        s_wready = sem("expert_weights_ready")
        s_xr = [sem("expert_rows_in_0"), sem("expert_rows_in_1")]
        s_xtr = sem("expert_rows_transposes_done")
        s_xec = sem("expert_rows_transposed_copied")
        s_h = sem("up_products_done")
        s_silu = sem("silu_done")
        s_hm = sem("hidden_ready")
        s_htr = sem("hidden_transposes_done")
        s_ht = sem("hidden_transposed_copied")
        s_y = sem("down_product_done")
        s_ya = sem("down_product_read")
        s_ys = [sem("expert_rows_out_0"), sem("expert_rows_out_1")]
        s_all_out = sem("all_expert_rows_out")
        s_gat = [sem(f"outputs_gathered_{b}") for b in range(NGATHER)]
        s_comb = sem("output_combined")
        s_store = sem("output_ready")
        s_done = sem("output_stored")
        s_dve = sem("dve_chain")
        s_act = sem("act_chain")
        s_pool = sem("pool_chain")
        s_sp = sem("sp_waits_passed")

        def rows_in(s, q):
            return 16 * (s // 2 + 1) if isinstance(s, int) else (s - q) * 8 + 16

        NP = T + KT

        def spread(a, shape):
            return a.unsqueeze(2).to_broadcast(shape)

        NTILE = H * T
        UN = 2 * T
        BODIES = NTILE // UN
        SU = SHARED * T

        block = ctx.enter_context(nc.Block())

        @block.sync
        def _(sp):
            sp.wait_ge(s_pad, 1)
            sp.dma_start(x_sb[:, 0:T - 1, :], x[0:(T - 1) * P, :].rearrange("(t p) d -> p t d", p=P)).then_inc(s_x, 16)
            sp.dma_start(x_sb[0:TAIL, T - 1, :], x[(T - 1) * P:NTOK, :]).then_inc(s_x, 16)
            sp.dma_start(w_qkv[:, 0, :, :], wq.rearrange("(k p) n -> p k n", p=P)).then_inc(s_wq, 16)
            sp.dma_start(bias_rows[:, 0, :], bq.unsqueeze(0).to_broadcast([P, D])).then_inc(s_small, 16)
            sp.dma_start(bias_rows[:, 1, :], bkv[0:D].unsqueeze(0).to_broadcast([P, D])).then_inc(s_small, 16)
            sp.dma_start(bias_rows[:, 2, :], bp.unsqueeze(0).to_broadcast([P, D])).then_inc(s_small, 16)
            sp.dma_start(gates[:, 0:1], g_xattn.unsqueeze(0).to_broadcast([P, 1])).then_inc(s_small, 16)
            sp.dma_start(gates[:, 1:2], g_ffn.unsqueeze(0).to_broadcast([P, 1])).then_inc(s_small, 16)
            with nc.allow_non_contiguous_dma(reason="512 words"):
                sp.dma_start(bv_col[:, :], bkv[D:2 * D].rearrange("(g p) -> p g", p=P)).then_inc(s_small, 16)
            sp.dma_start(wg_sb[:, :, :], wg_t).then_inc(s_small, 16)
            sp.dma_start(w_qkv[:, 1, :, :], wkv[:, 0:D].rearrange("(k p) n -> p k n", p=P)).then_inc(s_wk, 16)
            for k in range(DC):
                sp.dma_start(ctx_sb[:, k, 0:NKEY], ctx_t[:, k, :]).then_inc(s_ctx, 16)
            sp.dma_start(w_qkv[:, 2, :, :], wkv[:, D:2 * D].rearrange("(k p) n -> p k n", p=P)).then_inc(s_wv, 16)
            for t in range(T):
                sp.wait_ge(s_qi, t + 1)
                sp.dma_start_transpose(q_t[:, :, t * P:(t + 1) * P],
                                       parts[:, t % 2].rearrange("p h g d -> p (h g d)")).then_inc(s_qt[t % 2], 16)
            for j in range(T, NP):
                sp.wait_ge(s_parts, j - T + 1)
                kt = j - T
                sp.dma_start(key_parts[kt * P:(kt + 1) * P, :],
                             parts[:, j % 2].rearrange("p h g d -> p (h g d)")).then_inc(s_kp[j % 2], 16)
            sp.wait_ge(s_kp[T % 2], 16 * ((KT + 1) // 2))
            sp.wait_ge(s_kp[(T + 1) % 2], 16 * (KT // 2))
            for g in range(NG):
                sp.wait_ge(s_vb, g + 1)
                sp.dma_start_transpose(v_q[:, :, g * P:(g + 1) * P], v_b).then_inc(s_vq, 16)
            sp.dma_start(wp_sb, wp.rearrange("(k p) n -> p k n", p=P)).then_inc(s_wp, 16)

            def wait_tile(sem_, value):
                sp.wait_ge(sem_, value)
                sp.sem_inc(s_sp, 1)

            def load_keys(head, slot):
                sp.dma_start_transpose(k_t[slot].unsqueeze(1),
                                       key_parts[:, bass.ds(head * P, P)]).then_inc(s_kt[slot], 16)

            def transpose_p(n, k):
                wait_tile(s_conv, n - 1)
                if not isinstance(n, int) or n >= 4:
                    wait_tile(s_av, n - 3)
                sp.dma_start_transpose(p_t[k % 2], p_bf[k % 2]).then_inc(s_pt[k % 2], 16)

            def tiles(i, first, last):
                for k in range(UN):
                    n = i * UN + k
                    if not first or k >= 2:
                        transpose_p(n, k)
                    if k == 2:
                        if not first:
                            wait_tile(s_qb, NE * (i * UN))
                        load_keys(i * 2 + 1, 1)
                    if k == T + 2 and not last:
                        wait_tile(s_qb, NE * (i * UN + T))
                        load_keys(i * 2 + 2, 0)

            sp.wait_ge(s_vq, 16 * NG)
            sp.wait_ge(s_buf, 2)
            load_keys(0, 0)
            tiles(0, True, False)
            for i in range(1, BODIES - 1):
                tiles(i, False, False)
            tiles(BODIES - 1, False, True)
            for k in range(2):
                transpose_p(NTILE + k, k)

            def load_weights(n):
                slot = n % 2
                sp.dma_start(arena_a[:, slot * SLOT:slot * SLOT + UPC], w_up[n]).then_inc(s_win[slot], 16)
                sp.dma_start(arena_a[:, slot * SLOT + UPC:(slot + 1) * SLOT], w_down[n]).then_inc(s_win[slot], 16)

            sp.wait_ge(s_av, NTILE)
            def weights_ready(n):
                sp.wait_ge(s_win[n % 2], 32 * (n // 2 + 1))
                sp.sem_inc(s_wready, 1)

            load_weights(0)
            load_weights(1)
            weights_ready(0)
            for n in range(2, EX):
                weights_ready(n - 1)
                if n - 2 < SHARED:
                    sp.wait_ge(s_y, T * (n - 1))
                else:
                    if n - 2 == SHARED:
                        sp.wait_ge(s_slots, 1)
                    e = n - 2 - SHARED
                    sp.wait_ge(s_y, sp.value_load(end_step[0:1, e:e + 1], min_val=1, max_val=SU + MAXT))
                    sp.sem_inc(s_sp, 1)
                load_weights(n)
            weights_ready(EX - 1)
            for t in range(T):
                rows = P if t < T - 1 else TAIL
                sp.wait_ge(s_store, t + 1)
                sp.dma_start(out[t * P:t * P + rows, :], y_sb[0:rows, t, :]).then_inc(s_done, 16)
            sp.wait_ge(s_done, 16 * T)

        @block.tensor
        def _(pe):
            mm = nc.tensor.matmul

            def transpose_tokens(src, done, ready, wait_count, copied, base):
                for t in range(T):
                    pe.wait_ge(ready, wait_count(t))
                    if t >= 2:
                        pe.wait_ge(copied, base + t - 1)
                    for k in range(DC):
                        last = nc.tensor.transpose(ps[:, t % 2, k * P:(k + 1) * P],
                                                   src[:, t, k * P:(k + 1) * P], ident[:, :])
                    last.then_inc(done, 1)

            pe.wait_ge(s_ident, 1)
            transpose_tokens(xn, s_tr, s_xn, lambda t: t + 1, s_xt, 0)
            pe.wait_ge(s_wq, 16)
            for j in range(NP):
                if j < T:
                    pe.wait_ge(s_xt, j + 1)
                if j == T:
                    pe.wait_ge(s_wk, 16)
                    pe.wait_ge(s_ctx, 16 * DC)
                if j >= 2:
                    pe.wait_ge(s_pf, j - 1)
                for k in range(DC):
                    src = x_t[:, k, j * P:(j + 1) * P] if j < T else ctx_sb[:, k, (j - T) * P:(j - T + 1) * P]
                    last = mm(ps[:, 2 + j % 2, :], src, w_qkv[:, 0 if j < T else 1, k, :],
                              start=(k == 0), stop=(k == DC - 1))
                last.then_inc(s_proj, 1)
            pe.wait_ge(s_wv, 16)
            NV = (NKEY + BANK - 1) // BANK
            for v in range(NG * NV):
                g, c = divmod(v, NV)
                w = min(BANK, NKEY - c * BANK)
                if v >= 2:
                    pe.wait_ge(s_vf, v - 1)
                for k in range(DC):
                    last = mm(ps[:, 4 + v % 2, 0:w], w_qkv[:, 2, k, g * P:(g + 1) * P],
                              ctx_sb[:, k, c * BANK:c * BANK + w], start=(k == 0), stop=(k == DC - 1))
                last.then_inc(s_vps, 1)

            def products(i, k, span, bank):
                slot, t = divmod(k, T)
                for b in range(0, span[1], BANK):
                    a, w = span[0] + b, min(BANK, span[1] - b)
                    last = mm(ps[:, bank + b // BANK, 0:w], q_t[0:3 * HD, bass.ds(i * 2 + slot, 1), t * P:(t + 1) * P]
                              .rearrange("p h q -> p (h q)"), k_t[slot][0:3 * HD, a:a + w], start=True, stop=True)
                return last

            def for_max(i, n, k, j):
                slot, t = divmod(k, T)
                if t == 0 and j == 0:
                    pe.wait_ge(s_kt[slot], 16 * (i + 1))
                c = NM * n + j
                if not isinstance(c, int) or c >= 2:
                    pe.wait_ge(s_max, c - 1)
                products(i, k, MAX_SPANS[j], MAX_BANK[(NM * k + j) % 2]).then_inc(s_qa, 1)

            def for_exp(i, n, k, j):
                c = NE * n + j
                if not isinstance(c, int) or c >= 2:
                    pe.wait_ge(s_exp, c - 1)
                products(i, k, EXP_SPANS[j], EXP_BANK[(NE * k + j) % 2]).then_inc(s_qb, 1)

            def weigh_values(i, m, k):
                slot, t = divmod(k, T)
                head = i * 2 + slot
                pe.wait_ge(s_pt[k % 2], 16 * (i * (UN // 2) + k // 2 + 1))
                if not isinstance(m, int) or m >= 1:
                    pe.wait_ge(s_ao, m)
                for c in range(KT):
                    last = mm(ps[:, OUT_BANK, 0:HD], p_t[k % 2][:, c, :], v_q[:, c, bass.ds(head * HD, HD)],
                              start=(c == 0), stop=(c == KT - 1))
                last.then_inc(s_av, 1)

            def before_tile(i, k, d):
                return (i, k - d) if k >= d else (i - 1, k - d + UN)

            def turn(i, k, n):
                i1, k1 = before_tile(i, k, 1)
                i2, k2 = before_tile(i, k, 2)
                i4, k4 = before_tile(i, k, 4)
                known = isinstance(n, int)
                two, one, four = (not known or d <= n < NTILE + d for d in (2, 1, 4))
                if two:
                    for_exp(i2, n - 2, k2, 2)
                if one:
                    for_max(i1, n - 1, k1, 2)
                    for_exp(i1, n - 1, k1, 0)
                    for_max(i1, n - 1, k1, 3)
                    for_exp(i1, n - 1, k1, 1)
                if four:
                    weigh_values(i4, n - 4, k4)
                if not known or n < NTILE:
                    for_max(i, n, k, 0)
                    for_max(i, n, k, 1)

            pe.wait_ge(s_qt[0], 16 * ((T + 1) // 2))
            pe.wait_ge(s_qt[1], 16 * (T // 2))
            pe.wait_ge(s_vq, 16 * NG)
            for k in range(UN):
                turn(0, k, k)
            for i in range(1, BODIES):
                for k in range(UN):
                    turn(i, k, i * UN + k)
            for k in range(4):
                turn(BODIES, k, NTILE + k)

            transpose_tokens(attn, s_otr, s_attn, lambda t: 1, s_ot, 0)
            pe.wait_ge(s_wp, 16)
            for t in range(T):
                pe.wait_ge(s_ot, t + 1)
                if t >= 2:
                    pe.wait_ge(s_x1, t - 1)
                for k in range(DC):
                    last = mm(ps[:, 2 + t % 2, :], attn_t[:, k, t * P:(t + 1) * P], wp_sb[:, k, :],
                              start=(k == 0), stop=(k == DC - 1))
                last.then_inc(s_out, 1)
            transpose_tokens(xn, s_tr, s_xn, lambda t: T + t + 1, s_xt, T)
            pe.wait_ge(s_xt, 2 * T)
            for t in range(T):
                for k in range(DC):
                    last = mm(ps[:, 4, t * E:(t + 1) * E], x2_t[:, k, t * P:(t + 1) * P], wg_sb[:, k, :],
                              start=(k == 0), stop=(k == DC - 1))
            last.then_inc(s_lg, 1)

            pe.wait_ge(s_sel, 1)
            flat = lambda a: a.rearrange("p t e -> p (t e)")
            mm(ps[:, 5, 0:T * E], upper[:, :], flat(sel[:, :, :]), start=True, stop=False)
            mm(ps[:, 5, 0:T * E], ones[:, :], flat(sel_before[:, :, :]), start=False, stop=True)
            mm(ps[:, 6, 0:E], ones[:, :], sel_total[:, :], start=True, stop=True).then_inc(s_pos, 1)

            def up(src, col, q, w):
                for k in range(DC):
                    last = mm(ps[:, 1 + 2 * q + w, 0:INTER], src(k),
                              arena_a[:, bass.ds(col + (w * DC + k) * INTER, INTER)],
                              start=(k == 0), stop=(k == DC - 1))
                return last

            def transpose_hidden(u, q):
                pe.wait_ge(s_hm, u + 1)
                if not isinstance(u, int) or u >= 1:
                    pe.wait_ge(s_ht, u)
                for c in range(IC):
                    last = nc.tensor.transpose(ps[0:IW[c], 5, c * P:(c + 1) * P],
                                               h_mul[:, q, c * P:c * P + IW[c]], ident[:, :])
                last.then_inc(s_htr, 1)

            def down(u, col, q):
                pe.wait_ge(s_ht, u + 1)
                if not isinstance(u, int) or u >= 2:
                    pe.wait_ge(s_ya, u - 1)
                for c in range(IC):
                    last = mm(ps[:, 6 + q, :], h_t[0:IW[c], q, c * P:(c + 1) * P],
                              arena_a[0:IW[c], bass.ds(col + UPC + c * D, D)], start=(c == 0), stop=(c == IC - 1))
                last.then_inc(s_y, 1)

            def transpose_rows(s, q):
                pe.wait_ge(s_xr[q], rows_in(s, q))
                if not isinstance(s, int) or s >= 1:
                    pe.wait_ge(s_xec, s)
                for k in range(DC):
                    last = nc.tensor.transpose(ps[:, 0, k * P:(k + 1) * P], x_rows[:, q, k * P:(k + 1) * P],
                                               ident[:, :])
                last.then_inc(s_xtr, 1)

            for u in range(SU):
                part, t = divmod(u, T)
                q = u % 2
                if t == 0:
                    pe.wait_ge(s_wready, part + 1)
                src = lambda k: x2_t[:, k, t * P:(t + 1) * P]
                if u >= 2:
                    pe.wait_ge(s_hm, u - 1)
                up(src, (part % 2) * SLOT, q, 0)
                if u:
                    transpose_hidden(u - 1, 1 - q)
                up(src, (part % 2) * SLOT, q, 1).then_inc(s_h, 1)
                if u:
                    down(u - 1, ((u - 1) // T % 2) * SLOT, 1 - q)
            transpose_rows(0, 0)

            def routed(s, q, col, col_before):
                u = SU + s
                src = lambda k: xe_t[:, q, k, :]
                pe.wait_ge(s_xec, s + 1)
                pe.wait_ge(s_hm, u - 1)
                up(src, col, q, 0)
                transpose_hidden(u - 1, 1 - q)
                up(src, col, q, 1).then_inc(s_h, 1)
                transpose_rows(s + 1, 1 - q)
                down(u - 1, col_before, 1 - q)

            def column(s):
                return pe.value_load(weight_col[0:1, bass.ds(s, 1)], min_val=0, max_val=SLOT)

            def pair(b, first):
                s0, s1 = b * 2, b * 2 + 1
                before = ((SU - 1) // T % 2) * SLOT if first else column(s0 - 1)
                c0, c1 = column(s0), column(s1)
                need = [pe.value_load(weight_need[0:1, bass.ds(s, 1)], min_val=1, max_val=EX) for s in (s0, s1)]
                pe.wait_ge(s_wready, need[0])
                routed(s0, 0, c0, before)
                pe.wait_ge(s_wready, need[1])
                routed(s1, 1, c1, c0)

            pe.wait_ge(s_slots, 1)
            pairs = pe.value_load(n_pairs[0:1, 0:1], min_val=(MINT + 1) // 2, max_val=MAXT // 2)
            pair(0, True)
            with pe.Fori(1, pairs) as b:
                pair(b, False)
            last_column = column(pairs * 2 - 1)
            transpose_hidden(SU + pairs * 2 - 1, 1)
            down(SU + pairs * 2 - 1, last_column, 1)

        @block.scalar
        def _(act):
            chain = [0]

            def link(ins):
                chain[0] += 1
                ins.then_inc(s_act, 1)
                act.wait_ge(s_act, chain[0])

            act.wait_ge(s_var, 1)
            nc.scalar.activation(std[:, :], std[:, :], ACT.Sqrt).then_inc(s_std, 1)

            def copy_transposed(done, count, copied, dst, scale=None):
                for t in range(T):
                    act.wait_ge(done, count + t + 1)
                    src = ps[:, t % 2, :].rearrange("p (k q) -> p k q", k=DC)
                    if scale is None:
                        last = nc.scalar.copy(dst[:, :, t * P:(t + 1) * P], src)
                    else:
                        for k in range(DC):
                            last = nc.scalar.activation(dst[:, k, t * P:(t + 1) * P], src[:, k, :], ACT.Copy,
                                                        scale=scale[:, k:k + 1])
                    last.then_inc(copied, 1)

            copy_transposed(s_tr, 0, s_xt, x_t)
            for kt in range(KT):
                j = T + kt
                act.wait_ge(s_kd, kt + 1)
                if kt < 2:
                    act.wait_ge(s_qt[j % 2], 16 * ((T + 1 - j % 2) // 2))
                else:
                    act.wait_ge(s_kp[j % 2], 16 * (kt // 2))
                nc.scalar.copy(parts[:, j % 2, :, 0, :], proj_d[:, j % 2, :].rearrange("p (h d) -> p h d", h=H)
                               ).then_inc(s_hi, 1)
                act.wait_ge(s_rest, kt + 1)
                nc.scalar.copy(parts[:, j % 2, :, 1, :], proj_r[:, j % 2, :].rearrange("p (h d) -> p h d", h=H)
                               ).then_inc(s_mid, 1)
            act.wait_ge(s_small, 16 * 7)
            NV = (NKEY + BANK - 1) // BANK
            for v in range(NG * NV):
                g, c = divmod(v, NV)
                w = min(BANK, NKEY - c * BANK)
                act.wait_ge(s_vps, v + 1)
                if c == 0 and g:
                    act.wait_ge(s_vi, g)
                nc.scalar.activation(v_f[:, c * BANK:c * BANK + w], ps[:, 4 + v % 2, 0:w], ACT.Identity,
                                     bias=bv_col[:, g:g + 1]).then_inc(s_vf, 1)
            act.wait_ge(s_small, 16 * 7)
            nc.scalar.activation(gates[:, :], gates[:, :], ACT.Tanh).then_inc(s_gate, 1)

            def exps(i, n, k):
                slot, t = divmod(k, T)
                head = i * 2 + slot
                act.wait_ge(s_bias, n + 1)
                if not isinstance(n, int) or n >= 2:
                    act.wait_ge(s_conv, n - 1)
                for j, (a, w) in enumerate(EXP_SPANS):
                    act.wait_ge(s_qb, NE * n + j + 1)
                    bank = BANK * EXP_BANK[(NE * k + j) % 2]
                    nc.scalar.activation(p_int[k % 2][:, a:a + w], ps_flat[:, bank:bank + w],
                                         ACT.Exp, bias=exp_bias[:, k % 2:k % 2 + 1],
                                         scale=q_step[:, bass.ds(head, 1), t],
                                         accum_out=exp_sums[:, bass.ds(head, 1), t, j]).then_inc(s_exp, 1)

            def keep_output(i, m, k):
                slot, t = divmod(k, T)
                act.wait_ge(s_av, m + 1)
                nc.scalar.copy(attn[:, t, bass.ds((i * 2 + slot) * HD, HD)], ps[:, OUT_BANK, 0:HD]).then_inc(s_ao, 1)

            def tiles(i, first):
                for k in range(UN):
                    n = i * UN + k
                    exps(i, n, k)
                    if k >= 3:
                        keep_output(i, n - 3, k - 3)
                    elif not first:
                        keep_output(i - 1, n - 3, k - 3 + UN)

            act.wait_ge(s_buf, 2)
            tiles(0, True)
            for i in range(1, BODIES):
                tiles(i, False)
            for k in range(3):
                keep_output(BODIES - 1, NTILE - 3 + k, UN - 3 + k)

            copy_transposed(s_otr, 0, s_ot, attn_t, v_step)
            act.wait_ge(s_var, 2)
            nc.scalar.activation(std[:, :], std[:, :], ACT.Sqrt).then_inc(s_std, 1)
            copy_transposed(s_tr, T, s_xt, x2_t)
            act.wait_ge(s_lgc, 1)
            nc.scalar.activation(score[:, :, :], logit[:, :, :], ACT.Exp).then_inc(s_sc, 1)

            def silu(u, q):
                act.wait_ge(s_h, u + 1)
                nc.scalar.activation(h_act[:, q, 0:INTER], ps[:, 1 + 2 * q, 0:INTER], ACT.Silu).then_inc(s_silu, 1)

            def copy_hidden(u, q):
                act.wait_ge(s_htr, u + 1)
                for c in range(IC):
                    last = nc.scalar.copy(h_t[0:IW[c], q, c * P:(c + 1) * P], ps[0:IW[c], 5, c * P:(c + 1) * P])
                last.then_inc(s_ht, 1)

            def copy_rows(s, q):
                act.wait_ge(s_xtr, s + 1)
                nc.scalar.copy(xe_t[:, q, :, :], ps[:, 0, :].rearrange("p (k q) -> p k q", k=DC)).then_inc(s_xec, 1)

            act.wait_ge(s_xz, 32)
            for u in range(SU):
                if u:
                    copy_hidden(u - 1, (u - 1) % 2)
                silu(u, u % 2)
            copy_rows(0, 0)

            def routed(s, q):
                copy_hidden(SU + s - 1, 1 - q)
                silu(SU + s, q)
                copy_rows(s + 1, 1 - q)

            act.wait_ge(s_slots, 1)
            pairs = act.value_load(n_pairs[0:1, 0:1], min_val=(MINT + 1) // 2, max_val=MAXT // 2)
            with act.Fori(0, pairs) as b:
                for q in range(2):
                    routed(b * 2 + q, q)
            copy_hidden(SU + pairs * 2 - 1, 1)

        @block.vector
        def _(dve):
            v = nc.vector
            chain = [0]

            def link(ins):
                chain[0] += 1
                ins.then_inc(s_dve, 1)
                dve.wait_ge(s_dve, chain[0])

            def layer_norm(n):
                for t in range(T):
                    last = v.bn_stats(stats[:, t, :], x_sb[:, t, :])
                link(last)
                for t in range(T):
                    last = v.bn_aggr(mean_var[:, t, :], stats[:, t, :])
                link(last)
                v.tensor_scalar_add(std[:, :], mean_var[:, :, 1], LN_EPS).then_inc(s_var, 1)
                dve.wait_ge(s_std, n)
                link(v.reciprocal(std[:, :], std[:, :]))
                for t in range(T):
                    v.tensor_scalar(xn[:, t, :], x_sb[:, t, :], mean_var[:, t, 0:1], std[:, t:t + 1],
                                    ALU.subtract, ALU.mult).then_inc(s_xn, 1)

            dve.wait_ge(s_x, 32)
            layer_norm(1)

            dve.wait_ge(s_small, 16 * 7)
            for j in range(NP):
                b = j % 2
                kt = j - T
                pf = proj_f[:, b, :]
                heads = lambda a: a.rearrange("p (h d) -> p h d", h=H)
                dve.wait_ge(s_proj, j + 1)
                chain[0] += 1
                ins = v.tensor_tensor(pf, ps[:, 2 + b, :], bias_rows[:, 0 if j < T else 1, :], ALU.add)
                ins.then_inc(s_pf, 1)
                chain[0] -= 1
                dve.wait_ge(s_pf, j + 1)
                if j < T:
                    link(v.tensor_scalar(pf, pf, QSCALE, None, ALU.mult))
                link(v.tensor_reduce(amax[:, b, :], heads(pf), AX.X, ALU.max, apply_absolute_value=True))
                st = q_step[:, :, j] if j < T else step[:, b, :]
                link(v.tensor_scalar(st, amax[:, b, :], 1.0 / 127.0, 1e-8, ALU.mult, ALU.max))
                if j < T:
                    v.tensor_scalar(neg_q_step[:, :, j], st, -1.0, None, ALU.mult)
                link(v.reciprocal(inv_step[:, b, :], st))
                link(v.tensor_tensor(heads(proj_i[:, b, :]), heads(pf), spread(inv_step[:, b, :], [P, H, HD]), ALU.mult))
                if j < T:
                    if j >= 2:
                        dve.wait_ge(s_qt[b], 16 * (j // 2))
                    v.tensor_copy(parts[:, b].rearrange("p h g d -> p g h d"),
                                  proj_i[:, b, :].rearrange("p (h d) -> p h d", h=H).unsqueeze(1)
                                  .to_broadcast([P, HG, H, HD])).then_inc(s_qi, 1)
                else:
                    if kt >= 2:
                        dve.wait_ge(s_rest, kt - 1)
                        dve.wait_ge(s_hi, kt - 1)
                    v.tensor_tensor(heads(proj_d[:, b, :]), heads(proj_i[:, b, :]), spread(step[:, b, :], [P, H, HD]),
                                    ALU.mult).then_inc(s_kd, 1)

            NV = (NKEY + BANK - 1) // BANK
            for g in range(NG):
                dve.wait_ge(s_vf, NV * (g + 1))
                link(v.tensor_reduce(v_amax[:, g:g + 1], v_f[:, 0:NKEY], AX.X, ALU.max, apply_absolute_value=True))
                link(v.tensor_scalar(v_step[:, g:g + 1], v_amax[:, g:g + 1], 1.0 / 127.0, 1e-8, ALU.mult, ALU.max))
                link(v.reciprocal(v_inv[:, g:g + 1], v_step[:, g:g + 1]))
                if g:
                    dve.wait_ge(s_vq, 16 * g)
                else:
                    link(v.memset(v_i[:, NKEY:KPAD], 0))
                v.tensor_scalar(v_i[:, 0:NKEY], v_f[:, 0:NKEY], v_inv[:, g:g + 1], None, ALU.mult).then_inc(s_vi, 1)
                dve.wait_ge(s_vi, g + 1)
                v.tensor_copy(v_b[:, 0:NKEY], v_i[:, 0:NKEY]).then_inc(s_vb, 1)

            dve.wait_ge(s_vps, NG * NV)
            for i in range(2):
                v.memset(p_int[i][:, NKEY:KPAD], 0).then_inc(s_buf, 1)
            dve.wait_ge(s_buf, 2)

            def to_bf16(i, n, k):
                dve.wait_ge(s_exp, NE * (n - 1))
                if not isinstance(n, int) or n >= 4:
                    dve.wait_ge(s_pt[k % 2], 16 * (i * (UN // 2) + k // 2))
                v.tensor_copy(p_bf[k % 2], p_int[k % 2]).then_inc(s_conv, 1)

            def maximum(i, n, k, base):
                slot, t = divmod(k, T)
                for j, (a, w) in enumerate(MAX_SPANS):
                    dve.wait_ge(s_qa, NM * n + j + 1)
                    col = BANK * MAX_BANK[(NM * k + j) % 2]
                    v.tensor_reduce(span_max[:, k % 2, j:j + 1], ps_flat[:, col:col + w], AX.X, ALU.max
                                    ).then_inc(s_max, 1)
                dve.wait_ge(s_max, NM * n + NM)
                v.tensor_reduce(row_max[:, k % 2:k % 2 + 1], span_max[:, k % 2, :], AX.X, ALU.max).then_inc(s_dve, 1)
                dve.wait_ge(s_dve, base + n + 1)
                v.tensor_scalar(exp_bias[:, k % 2:k % 2 + 1], row_max[:, k % 2:k % 2 + 1],
                                neg_q_step[:, bass.ds(i * 2 + slot, 1), t], LOG255, ALU.mult, ALU.add
                                ).then_inc(s_bias, 1)

            def tiles(i, first, base):
                for k in range(UN):
                    n = i * UN + k
                    if k >= 2:
                        to_bf16(i, n, k - 2)
                    elif not first:
                        to_bf16(i - 1, n, k - 2 + UN)
                    maximum(i, n, k, base)

            base = chain[0]
            tiles(0, True, base)
            for i in range(1, BODIES):
                tiles(i, False, base)
            chain[0] = base + NTILE
            for k in range(2):
                to_bf16(BODIES - 1, NTILE + k, UN - 2 + k)

            dve.wait_ge(s_exp, NE * NTILE)
            link(v.tensor_reduce(inv_sum[:, :, :], exp_sums[:, :, :, :], AX.X, ALU.add))
            link(v.reciprocal(inv_sum[:, :, :], inv_sum[:, :, :]))
            link(v.tensor_scalar(inv_sum[:, :, :], inv_sum[:, :, :], 1e-8, None, ALU.max))
            dve.wait_ge(s_ao, NTILE)
            for t in range(T):
                a = attn[:, t, :].rearrange("p (h d) -> p h d", h=H)
                last = v.tensor_tensor(a, a, spread(inv_sum[:, :, t], [P, H, HD]), ALU.mult)
            last.then_inc(s_attn, 1)

            dve.wait_ge(s_gate, 1)
            for t in range(T):
                dve.wait_ge(s_out, t + 1)
                link(v.tensor_tensor(proj_f[:, 0, :], ps[:, 2 + t % 2, :], bias_rows[:, 2, :], ALU.add))
                v.scalar_tensor_tensor(x_sb[:, t, :], proj_f[:, 0, :], gates[:, 0:1], x_sb[:, t, :],
                                       ALU.mult, ALU.add).then_inc(s_x1, 1)
                dve.wait_ge(s_x1, t + 1)
            layer_norm(2)

            dve.wait_ge(s_lg, 1)
            link(v.tensor_copy(logit[:, :, :], ps[:, 4, 0:T * E].rearrange("p (t e) -> p t e", t=T)))
            link(v.tensor_reduce(tok[:, :], logit[:, :, :], AX.X, ALU.max))
            v.tensor_tensor(logit[:, :, :], logit[:, :, :], spread(tok[:, :], [P, T, E]), ALU.subtract).then_inc(s_lgc, 1)
            dve.wait_ge(s_sc, 1)
            link(v.tensor_reduce(tok[:, :], score[:, :, :], AX.X, ALU.add))
            link(v.reciprocal(tok[:, :], tok[:, :]))
            link(v.tensor_tensor(score[:, :, :], score[:, :, :], spread(tok[:, :], [P, T, E]), ALU.mult))
            link(v.tensor_reduce(grp[:, :, :], score[:, :, :].rearrange("p t (g e) -> p t g e", g=EG), AX.X, ALU.max))

            def ranks(dst, a, n, mask, tmp, eq):
                shape = [P, T, n, n]
                other, own = a.unsqueeze(2).to_broadcast(shape), a.unsqueeze(3).to_broadcast(shape)
                v.tensor_tensor(tmp, other, own, ALU.is_gt)
                link(v.tensor_tensor(eq, other, own, ALU.is_equal))
                link(v.tensor_tensor(eq, eq, mask.unsqueeze(1).to_broadcast(shape), ALU.mult))
                link(v.tensor_tensor(tmp, tmp, eq, ALU.add))
                link(v.tensor_reduce(dst, tmp, AX.X, ALU.add))

            small = lambda a: a.rearrange("p t e f -> p (t e f)")[:, 0:T * EG * EG].rearrange(
                "p (t e f) -> p t e f", t=T, e=EG)
            dve.wait_ge(s_pool, 8)
            dve.wait_ge(s_av, NTILE)
            ranks(grp_rank[:, :, :], grp[:, :, :], EG, before_g[:, :, :], small(rank_tmp), small(rank_eq))
            link(v.tensor_scalar(grp[:, :, :], grp_rank[:, :, :], TOPG - 0.5, None, ALU.is_lt))
            link(v.tensor_scalar(grp_rank[:, :, :], grp[:, :, :], -1.0, None, ALU.add))
            by_group = lambda a: a.rearrange("p t (g e) -> p t g e", g=EG)
            gs = [P, T, EG, E // EG]
            link(v.tensor_tensor(by_group(logit[:, :, :]), by_group(score[:, :, :]),
                                 grp[:, :, :].unsqueeze(3).to_broadcast(gs), ALU.mult))
            link(v.tensor_tensor(by_group(logit[:, :, :]), by_group(logit[:, :, :]),
                                 grp_rank[:, :, :].unsqueeze(3).to_broadcast(gs), ALU.add))
            ranks(rank[:, :, :], logit[:, :, :], E, before[:, :, :], rank_tmp, rank_eq)
            link(v.tensor_scalar(sel[:, :, :], rank[:, :, :], TOPK - 0.5, None, ALU.is_lt))
            link(v.tensor_scalar(sel[:, T - 1, :], sel[:, T - 1, :], valid[:, 0:1], None, ALU.mult))
            link(v.memset(sel_before[:, 0, :], 0.0))
            for t in range(1, T):
                link(v.tensor_tensor(sel_before[:, t, :], sel_before[:, t - 1, :], sel[:, t - 1, :], ALU.add))
            v.tensor_tensor(sel_total[:, :], sel_before[:, T - 1, :], sel[:, T - 1, :], ALU.add).then_inc(s_sel, 1)
            for j in range(TOPK):
                link(v.scalar_tensor_tensor(pick[:, :, :], rank[:, :, :], float(j), score[:, :, :],
                                            ALU.is_equal, ALU.mult))
                link(v.tensor_reduce(weight_j[:, j, :], pick[:, :, :], AX.X, ALU.add))
            dve.wait_ge(s_pos, 1)
            link(v.tensor_copy(count[:, :], ps[:, 6, 0:E]))
            shape = [P, E, T - 1]
            link(v.tensor_tensor(over[:, :, :], count[:, :].unsqueeze(2).to_broadcast(shape),
                                 thresholds[:, :].unsqueeze(1).to_broadcast(shape), ALU.is_gt))
            link(v.tensor_reduce(tiles_of[:, :], over[:, :, :], AX.X, ALU.add))
            link(v.tensor_scalar(tiles_of[:, :], tiles_of[:, :], 1.0, None, ALU.add))
            link(v.tensor_tensor(prefix[:, :, :], before[:, :, :],
                                 tiles_of[:, :].unsqueeze(1).to_broadcast([P, E, E]), ALU.mult))
            link(v.tensor_reduce(first_tile[:, :], prefix[:, :, :], AX.X, ALU.add))
            link(v.tensor_tensor(end_tile[:, :], first_tile[:, :], tiles_of[:, :], ALU.add))
            link(v.tensor_scalar(end_step[:, :], end_tile[:, :], float(SU), None, ALU.add))
            for less in range(2):
                link(v.tensor_scalar(n_pairs[:, less:less + 1], end_tile[:, E - 1:E], 0.5, 0.25 - less, ALU.mult, ALU.add))
            link(v.tensor_scalar(first_tile[:, :], first_tile[:, :], float(P), None, ALU.mult))
            link(v.tensor_tensor(slot_of[:, :, :], ps[:, 5, 0:T * E].rearrange("p (t e) -> p t e", t=T),
                                 first_tile[:, :].unsqueeze(1).to_broadcast([P, T, E]), ALU.add))
            for j in range(TOPK):
                link(v.scalar_tensor_tensor(pick[:, :, :], rank[:, :, :], float(j), slot_of[:, :, :],
                                            ALU.is_equal, ALU.mult))
                link(v.tensor_reduce(slot_j[:, j, :], pick[:, :, :], AX.X, ALU.add))
            link(v.tensor_copy(slot_i[:, :, :], slot_j[:, :, :]))
            shape = [P, MAXT, E]
            link(v.tensor_tensor(past[:, :, :], end_tile[:, :].unsqueeze(1).to_broadcast(shape),
                                 tile_no[:, :].unsqueeze(2).to_broadcast(shape), ALU.is_le))
            link(v.tensor_reduce(tile_expert[:, :], past[:, :, :], AX.X, ALU.add))
            link(v.tensor_scalar(tile_expert[:, :], tile_expert[:, :], float(E - 1), None, ALU.min))
            link(v.tensor_scalar(weight_need[:, :], tile_expert[:, :], float(SHARED + 1), None, ALU.add))
            link(v.tensor_scalar(weight_col[:, :], tile_expert[:, :], 0.5, -0.25, ALU.mult, ALU.add))
            link(v.tensor_scalar(tile_tmp[:, :], weight_col[:, :], -2.0, None, ALU.mult))
            link(v.tensor_tensor(tile_tmp[:, :], tile_tmp[:, :], tile_expert[:, :], ALU.add))
            v.tensor_scalar(weight_col[:, :], tile_tmp[:, :], float(SLOT), None, ALU.mult).then_inc(s_slots, 1)

            def gate(u, q):
                dve.wait_ge(s_silu, u + 1)
                if not isinstance(u, int) or u >= 2:
                    dve.wait_ge(s_htr, u - 1)
                v.tensor_tensor(h_mul[:, q, 0:INTER], ps[:, 2 + 2 * q, 0:INTER], h_act[:, q, 0:INTER],
                                ALU.mult).then_inc(s_hm, 1)

            def keep_shared(u):
                part, t = divmod(u, T)
                dve.wait_ge(s_y, u + 1)
                if part == 0:
                    v.tensor_copy(y_sb[:, t, :], ps[:, 6 + u % 2, :]).then_inc(s_ya, 1)
                else:
                    dve.wait_ge(s_ya, u)
                    v.tensor_tensor(y_sb[:, t, :], ps[:, 6 + u % 2, :], y_sb[:, t, :], ALU.add).then_inc(s_ya, 1)

            def keep_routed(s, q, stored):
                dve.wait_ge(s_y, SU + s + 1)
                if stored is not None:
                    dve.wait_ge(s_ys[q], stored)
                v.tensor_copy(y_rows[:, q, :], ps[:, 6 + (SU + q) % 2, :]).then_inc(s_ya, 1)

            for u in range(SU):
                gate(u, u % 2)
                if u:
                    keep_shared(u - 1)
            gate(SU, 0)
            keep_shared(SU - 1)
            gate(SU + 1, 1)
            keep_routed(0, 0, None)
            pairs = dve.value_load(n_pairs[0:1, 0:1], min_val=(MINT + 1) // 2, max_val=MAXT // 2)

            def keep_pair(b, first):
                gate(SU + b * 2, 0)
                keep_routed(b * 2 - 1, 1, None if first else (b - 1) * 16)
                gate(SU + b * 2 + 1, 1)
                keep_routed(b * 2, 0, b * 16)

            before_last = dve.value_load(n_pairs[0:1, 1:2], min_val=(MINT + 1) // 2 - 1, max_val=MAXT // 2 - 1)
            keep_pair(1, True)
            with dve.Fori(2, pairs) as b:
                keep_pair(b, False)
            keep_routed(pairs * 2 - 1, 1, before_last * 16)

            for n in range(T * TOPK):
                t, j = divmod(n, TOPK)
                rows = P if t < T - 1 else TAIL
                dve.wait_ge(s_gat[n % NGATHER], 16 * (n // NGATHER + 1))
                if n == 0:
                    dve.wait_ge(s_ya, SU)
                if j:
                    dve.wait_ge(s_comb, n)
                v.scalar_tensor_tensor(y_sb[0:rows, t, :], gathered[0:rows, n % NGATHER, :], weight_j[0:rows, j, t:t + 1],
                                       y_sb[0:rows, t, :], ALU.mult, ALU.add).then_inc(s_comb, 1)
                if j == TOPK - 1:
                    dve.wait_ge(s_comb, n + 1)
                    v.scalar_tensor_tensor(y_sb[0:rows, t, :], y_sb[0:rows, t, :], gates[0:rows, 1:2],
                                           x_sb[0:rows, t, :], ALU.mult, ALU.add).then_inc(s_store, 1)

        @block.gpsimd
        def _(pool):
            p = nc.gpsimd
            p.memset(x_sb[:, T - 1, :], 0.0).then_inc(s_pad, 1)
            p.memset(ctx_sb[:, :, NKEY:KPAD], 0.0).then_inc(s_pool, 1)
            p.memset(ident[:, :], 0.0).then_inc(s_pool, 1)
            pool.wait_ge(s_pool, 2)
            p.affine_select(out=ident[:, :], in_=ident[:, :], compare_op=ALU.not_equal, fill=1.0, base=0,
                            pattern=[[-1, P]], channel_multiplier=1).then_inc(s_ident, 1)
            p.memset(before[:, :, :], 1.0).then_inc(s_pool, 1)
            pool.wait_ge(s_pool, 3)
            p.affine_select(out=before[:, :, :], in_=before[:, :, :], compare_op=ALU.is_gt, fill=0.0, base=0,
                            pattern=[[1, E], [-1, E]], channel_multiplier=0).then_inc(s_pool, 1)
            p.memset(before_g[:, :, :], 1.0).then_inc(s_ident, 1)
            pool.wait_ge(s_ident, 2)
            p.affine_select(out=before_g[:, :, :], in_=before_g[:, :, :], compare_op=ALU.is_gt, fill=0.0, base=0,
                            pattern=[[1, EG], [-1, EG]], channel_multiplier=0).then_inc(s_pool, 1)
            p.memset(ones[:, :], 1.0).then_inc(s_pool, 1)
            pool.wait_ge(s_pool, 6)
            p.affine_select(out=upper[:, :], in_=ones[:, :], compare_op=ALU.is_gt, fill=0.0, base=0,
                            pattern=[[1, P]], channel_multiplier=-1).then_inc(s_pool, 1)
            p.affine_select(out=valid[:, :], in_=ones[:, 0:1], compare_op=ALU.is_gt, fill=0.0, base=TAIL,
                            pattern=[[0, 1]], channel_multiplier=-1).then_inc(s_zero, 1)
            p.iota(iota_i[:, :], [[1, MAXT]], base=0, channel_multiplier=0).then_inc(s_zero, 1)
            pool.wait_ge(s_zero, 2)
            p.tensor_copy(tile_no[:, :], iota_i[:, :]).then_inc(s_zero, 1)
            pool.wait_ge(s_zero, 3)
            p.tensor_scalar(thresholds[:, :], tile_no[:, 1:T], float(P), None, ALU.mult).then_inc(s_pool, 1)
            for kt in range(KT):
                j = T + kt
                b = j % 2
                heads = lambda a: a.rearrange("p (h d) -> p h d", h=H)
                pool.wait_ge(s_kd, kt + 1)
                pool.wait_ge(s_hi, kt + 1)
                p.tensor_tensor(heads(proj_r[:, b, :]), heads(proj_d[:, b, :]), parts[:, b, :, 0, :],
                                ALU.subtract).then_inc(s_rest, 1)
                pool.wait_ge(s_rest, kt + 1)
                pool.wait_ge(s_mid, kt + 1)
                p.tensor_tensor(parts[:, b, :, 2, :], heads(proj_r[:, b, :]), parts[:, b, :, 1, :],
                                ALU.subtract).then_inc(s_parts, 1)

            pool.wait_ge(s_mid, KT)
            pool.wait_ge(s_parts, KT)
            p.memset(proj_r[:, 0, :], 0.0).then_inc(s_zero, 1)
            pool.wait_ge(s_zero, 4)
            pool.dma_start(expert_in.rearrange("(n p) d -> p n d", p=P),
                           proj_r[:, 0, :].unsqueeze(1).to_broadcast([P, MAXT + 1, D])).then_inc(s_xz, 16)
            pool.dma_start(expert_out[MINT * P:, :].rearrange("(n p) d -> p n d", p=P),
                           proj_r[:, 0, :].unsqueeze(1).to_broadcast([P, MAXT + 1 - MINT, D])).then_inc(s_xz, 16)

            pool.wait_ge(s_slots, 1)
            pool.wait_ge(s_xz, 32)
            for n in range(T * TOPK):
                t, j = divmod(n, TOPK)
                rows = P if t < T - 1 else TAIL
                p.indirect_dma_start(out=expert_in, out_offset=bass.IndirectOffsetOnAxis(ap=slot_i[0:rows, j, t:t + 1], axis=0),
                                     in_=xn[0:rows, t, :], in_offset=None).then_inc(s_scat[j], 16)
            for j in range(TOPK):
                pool.wait_ge(s_scat[j], 16 * T)

            def load_rows(s, q):
                pool.dma_start(x_rows[:, q, :], expert_in[bass.ds(s * P, P), :]).then_inc(s_xr[q], 16)

            def store_rows(s, q):
                pool.wait_ge(s_ya, SU + s + 1)
                pool.dma_start(expert_out[bass.ds(s * P, P), :], y_rows[:, q, :]).then_inc(s_ys[q], 16)

            load_rows(0, 0)
            load_rows(1, 1)
            pairs = pool.value_load(n_pairs[0:1, 0:1], min_val=(MINT + 1) // 2, max_val=MAXT // 2)
            with pool.Fori(0, pairs) as b:
                for q in range(2):
                    s = b * 2 + q
                    pool.wait_ge(s_xtr, s + 1)
                    load_rows(s + 2, q)
                    store_rows(s, q)
            for q in range(2):
                pool.wait_ge(s_ys[q], pairs * 16)
                pool.sem_inc(s_all_out, 1)
            for n in range(T * TOPK):
                t, j = divmod(n, TOPK)
                rows = P if t < T - 1 else TAIL
                if n >= NGATHER:
                    pool.wait_ge(s_comb, n - NGATHER + 1)
                p.indirect_dma_start(out=gathered[0:rows, n % NGATHER, :], out_offset=None, in_=expert_out,
                                     in_offset=bass.IndirectOffsetOnAxis(ap=slot_i[0:rows, j, t:t + 1], axis=0)
                                     ).then_inc(s_gat[n % NGATHER], 16)


def kernel(**inputs):
    import numpy as _np
    import concourse.bacc as _bacc
    from concourse import mybir as _mybir
    from concourse.bass_utils import run_bass_kernel_spmd as _run

    P = 128
    a = {k: _np.asarray(v) for k, v in inputs.items()}
    x, ctx = a["x"], a["ctx_2048"]
    D = x.shape[-1]
    DC = D // P
    w1, w3, w2 = a["L0_ffn_W1"], a["L0_ffn_W3"], a["L0_ffn_W2"]
    E, I = w1.shape[:2]
    s1 = a["L0_ffn_Ws1"].reshape(-1, I, D)
    s3 = a["L0_ffn_Ws3"].reshape(-1, I, D)
    s2 = a["L0_ffn_Ws2"].reshape(D, -1, I).transpose(1, 0, 2)
    IC = (I + P - 1) // P

    def up(w):
        return w.reshape(-1, I, DC, P).transpose(0, 3, 2, 1)

    def down(w):
        full = _np.zeros((w.shape[0], IC * P, D), w.dtype)
        full[:, :I] = w.transpose(0, 2, 1)
        return full.reshape(-1, IC, P, D).transpose(0, 2, 1, 3)

    ups = _np.stack([_np.concatenate([up(s1), up(w1)]), _np.concatenate([up(s3), up(w3)])], axis=2)
    downs = _np.concatenate([down(s2), down(w2)])
    laid = {
        "x": x.reshape(-1, D),
        "ctx_t": ctx.reshape(-1, DC, P).transpose(2, 1, 0),
        "g_xattn": a["g_xattn"],
        "g_ffn": a["g_ffn"],
        "wq": a["L0_xattn_Wq"],
        "bq": a["L0_xattn_bq"],
        "wkv": a["L0_xattn_Wkv"],
        "bkv": a["L0_xattn_bkv"],
        "wp": a["L0_xattn_Wp"],
        "bp": a["L0_xattn_bp"],
        "wg_t": a["L0_ffn_Wg"].reshape(E, DC, P).transpose(2, 1, 0),
        "w_up": ups.reshape(ups.shape[0], P, -1),
        "w_down": downs.reshape(downs.shape[0], P, -1),
    }
    laid = {k: _np.ascontiguousarray(v) for k, v in laid.items()}
    nc = _bacc.Bacc("TRN2", target_bir_lowering=False, num_devices=1)
    args = [nc.dram_tensor(f"in_{k}", v.shape, _mybir.dt.from_np(v.dtype), kind="ExternalInput").ap()
            for k, v in laid.items()]
    args.append(nc.dram_tensor("out_0", laid["x"].shape, _mybir.dt.float32, kind="ExternalOutput").ap())
    gated_xattn_moe_kernel(nc, *args)
    r = _run(nc, [{f"in_{k}": v for k, v in laid.items()}], core_ids=[0])
    return r.results[0]["out_0"].reshape(x.shape)
```

```python
import math
from contextlib import ExitStack

import concourse.bass as bass
from concourse import mybir


def gated_xattn_moe_kernel(
    nc: bass.Bass,
    x: bass.AP,
    ctx_t: bass.AP,
    g_xattn: bass.AP,
    g_ffn: bass.AP,
    wq: bass.AP,
    bq: bass.AP,
    wkv: bass.AP,
    bkv: bass.AP,
    wp: bass.AP,
    bp: bass.AP,
    wg_t: bass.AP,
    w_up: bass.AP,
    w_down: bass.AP,
    out: bass.AP,
):
    f32, bf16, i16 = mybir.dt.float32, mybir.dt.bfloat16, mybir.dt.int16
    ALU, ACT, AX = mybir.AluOpType, mybir.ActivationFunctionType, mybir.AxisListType

    P = 128
    NTOK, D = x.shape
    DC = D // P
    NKEY = ctx_t.shape[2]
    H, HD = 16, 32
    HG = P // HD
    NG = H // HG
    T = (NTOK + P - 1) // P
    TAIL = NTOK - (T - 1) * P
    KT = (NKEY + P - 1) // P
    KPAD = KT * P
    E = wg_t.shape[2]
    EX = w_up.shape[0]
    INTER = w_up.shape[2] // (2 * DC)
    IC = w_down.shape[2] // D
    IW = [min(P, INTER - P * c) for c in range(IC)]
    EG, TOPG, TOPK = 4, 2, 4
    SHARED = EX - E
    MAXT = (NTOK * TOPK - E) // P + E + 1
    MINT = NTOK * TOPK // P
    SU = SHARED * T
    PRE = 8
    POST = SU - PRE

    def shared_step(u):
        if u < PRE - T:
            return 0, u
        return (1, u - (PRE - T)) if u < PRE else (0, u - T)

    COMBINED = [[], [], [0], [1, 2], [3], [4], [5, 6]]
    POS_STEP = 3
    POS, TOT = 0, T * E
    LN_EPS = 1e-5
    QSCALE = 1.0 / math.sqrt(HD)
    LOG255 = math.log(255.0)
    BANK = 512

    BANK_SPANS = lambda banks: [(a * BANK, min(b * BANK, NKEY) - a * BANK) for a, b in zip(banks, banks[1:])]
    MAX_SPANS, MAX_BANK = BANK_SPANS([0, 2, 3, 5, 6]), [0, 2]
    EXP_SPANS, EXP_BANK = BANK_SPANS([0, 2, 4, 6]), [3, 5]
    NM, NE, OUT_BANK = len(MAX_SPANS), len(EXP_SPANS), 7

    ctx = ExitStack()
    with ctx:
        def sb(name, shape, dt):
            return ctx.enter_context(nc.sbuf_tensor(name, shape, dt))

        def sem(name):
            return ctx.enter_context(nc.semaphore(name))

        key_parts = nc.dram_tensor("key_parts", [KPAD, H * P], bf16, kind="Internal").ap()

        expert_in = nc.dram_tensor("expert_in", [(MAXT + 1) * P, D], f32, kind="Internal").ap()
        expert_out = nc.dram_tensor("expert_out", [(MAXT + 1) * P, D], f32, kind="Internal").ap()

        ZEROED = [(expert_in, a) for a in range(MAXT + 1)]
        ZEROED += [(expert_out, a) for a in range(MINT, MAXT + 1)]

        arena_a = sb("arena_a", [P, DC * KPAD], f32)
        arena_b = sb("arena_b", [P, 4608], f32)
        x_sb = sb("x_sb", [P, T, D], f32)
        w_qkv = sb("w_qkv", [P, 3, DC, D], f32)
        bias_rows = sb("bias_rows", [P, 3, D], f32)
        bv_col = sb("bv_col", [P, NG], f32)
        xt = sb("xt", [P, T * D], f32)
        q_t = sb("q_t", [P, H, T * P], bf16)
        v_q = sb("v_q", [P, KT, D], bf16)
        proj_f = sb("proj_f", [P, 2, D], f32)
        proj_i = sb("proj_i", [P, 2, D], i16)
        proj_d = sb("proj_d", [P, 2, D], f32)
        proj_r = sb("proj_r", [P, 2, D], f32)
        parts = sb("parts", [P, 2, H, HG, HD], bf16)
        ident = sb("ident", [P, P], f32)
        gates = sb("gates", [P, 2], f32)
        wg_sb = sb("wg_sb", [P, DC, E], f32)
        stats = sb("stats", [P, T, 6], f32)
        mean_var = sb("mean_var", [P, T, 2], f32)
        std = sb("std", [P, T], f32)
        amax = sb("amax", [P, 2, H], f32)
        step = sb("step", [P, 2, H], f32)
        inv_step = sb("inv_step", [P, 2, H], f32)
        v_amax = sb("v_amax", [P, NG], f32)
        v_part = sb("v_part", [P, (NKEY + BANK - 1) // BANK], f32)
        v_step = sb("v_step", [P, NG], f32)
        v_inv = sb("v_inv", [P, NG], f32)
        q_step = sb("q_step", [P, H, T], f32)
        tail_step = sb("tail_step", [P, NG], f32)
        neg_tail_step = sb("neg_tail_step", [P, NG], f32)
        tail_sums = sb("tail_sums", [P, NG, NE], f32)
        tail_inv = sb("tail_inv", [P, NG], f32)
        neg_q_step = sb("neg_q_step", [P, H, T], f32)
        span_max = sb("span_max", [P, 2, NM], f32)
        row_max = sb("row_max", [P, 2], f32)
        exp_bias = sb("exp_bias", [P, 2], f32)
        exp_sums = sb("exp_sums", [P, H, T, NE], f32)
        inv_sum = sb("inv_sum", [P, H, T], f32)
        logit = sb("logit", [P, T, E], f32)
        score = sb("score", [P, T, E], f32)
        tok = sb("tok", [P, T], f32)
        grp = sb("grp", [P, T, EG], f32)
        grp_rank = sb("grp_rank", [P, T, EG], f32)
        rank = sb("rank", [P, T, E], f32)
        sel = sb("sel", [P, T, E], f32)
        sel_before = sb("sel_before", [P, T, E], f32)
        sel_total = sb("sel_total", [P, E], f32)
        slot_of = sb("slot_of", [P, T, E], f32)
        slot_j = sb("slot_j", [P, TOPK, T], f32)
        slot_i = sb("slot_i", [P, TOPK, T], mybir.dt.int32)
        weight_j = sb("weight_j", [P, TOPK, T], f32)
        valid = sb("valid", [P, 1], f32)
        count = sb("count", [P, E], f32)
        thresholds = sb("thresholds", [P, T - 1], f32)
        tiles_of = sb("tiles_of", [P, E], f32)
        first_tile = sb("first_tile", [P, E], f32)
        end_tile = sb("end_tile", [P, E], f32)
        tile_no = sb("tile_no", [P, MAXT], f32)
        tile_expert = sb("tile_expert", [P, MAXT], f32)
        tile_tmp = sb("tile_tmp", [P, MAXT], f32)
        n_pairs = sb("n_pairs", [P, 2], mybir.dt.int32)
        weight_col = sb("weight_col", [P, MAXT], mybir.dt.int32)
        weight_need = sb("weight_need", [P, MAXT], mybir.dt.int32)
        end_step = sb("end_step", [P, E], mybir.dt.int32)
        iota_i = sb("iota_i", [P, MAXT], mybir.dt.int32)
        upper = sb("upper", [P, P], f32)
        ones = sb("ones", [P, P], f32)
        before = sb("before", [P, E, E], f32)
        before_g = sb("before_g", [P, EG, EG], f32)

        ps = ctx.enter_context(nc.psum_tensor("ps", [P, 8, BANK], f32))
        ps_flat = ps[:, :, :].rearrange("p b n -> p (b n)")

        ctx_sb = arena_a[:, :].rearrange("p (k n) -> p k n", k=DC)

        def bf_view(a, cols):
            return arena_a[:, a:a + cols // 2].bitcast(bf16)

        half = KPAD // 2
        k_t = [w_qkv[:, 1 + i, :, :].rearrange("p k n -> p (k n)").bitcast(bf16)[:, 0:KPAD] for i in range(2)]
        k_t[1:1] = [bf_view(half * i, KPAD) for i in range(2)]
        k_t += [arena_b[:, half * i:half * (i + 1)].bitcast(bf16) for i in range(2)]
        NK = len(k_t)
        attn_tail = bias_rows[:, 0, 0:NG * HD].rearrange("p (g d) -> p g d", g=NG)
        p_int = [arena_a[:, half * (2 + i):half * (3 + i)].bitcast(i16) for i in range(2)]
        p_bf = [bf_view(half * (4 + i), KPAD) for i in range(2)]
        p_t = [bf_view(half * (6 + i), KPAD).rearrange("p (c q) -> p c q", q=P) for i in range(2)]
        UPC, DNC = 2 * DC * INTER, IC * D
        SLOT = UPC + DNC
        x_rows = xt[:, 0:2 * D].rearrange("p (b d) -> p b d", b=2)
        xe_t = xt[:, 2 * D:4 * D].rearrange("p (b k q) -> p b k q", b=2, k=DC)
        y_rows = xt[:, 4 * D:6 * D].rearrange("p (b d) -> p b d", b=2)
        xn = arena_b[:, 0:T * D].rearrange("p (t d) -> p t d", t=T)
        v_f = arena_b[:, 0:KPAD]
        v_i = arena_b[:, KPAD:KPAD + half].bitcast(i16)
        v_b = arena_b[:, KPAD:KPAD + half].bitcast(bf16)
        v_fs = [v_f, xt[:, 0:KPAD]]
        x_t = xt[:, :].rearrange("p (k q) -> p k q", k=DC)
        attn = xt[:, :].rearrange("p (t d) -> p t d", t=T)
        q_f32 = q_t[:, :, :].rearrange("p h q -> p (h q)").bitcast(f32)
        attn_t = q_f32[:, 0:DC * T * P].rearrange("p (k q) -> p k q", k=DC)
        x2_t = q_f32[:, DC * T * P:2 * DC * T * P].rearrange("p (k q) -> p k q", k=DC)
        y_sb = v_q[:, :, :].rearrange("p c d -> p (c d)").bitcast(f32)[:, 0:T * D].rearrange("p (t d) -> p t d", t=T)
        wp_sb = w_qkv[:, 0, :, :]
        h_act = proj_f
        h_mul = proj_d
        h_t = proj_r
        v_q32 = v_q[:, :, :].rearrange("p c d -> p (c d)").bitcast(f32)
        rank_tmp = arena_a[:, 2 * SLOT:2 * SLOT + T * E * E].rearrange("p (t e f) -> p t e f", t=T, e=E)
        rank_eq = v_q32[:, T * D:T * D + T * E * E].rearrange("p (t e f) -> p t e f", t=T, e=E)
        part_words = parts[:, :, :, :, :].rearrange("p b h g d -> p (b h g d)").bitcast(f32)
        past = part_words[:, 0:MAXT * E].rearrange("p (s e) -> p s e", e=E)
        prefix = part_words[:, MAXT * E:(MAXT + E) * E].rearrange("p (e f) -> p e f", f=E)
        over = part_words[:, (MAXT + E) * E:(MAXT + E + T - 1) * E].rearrange("p (e t) -> p e t", e=E)
        pick = part_words[:, (MAXT + E + T - 1) * E:(MAXT + E + 2 * T - 1) * E].rearrange("p (t e) -> p t e", e=E)
        NGATHER = 8
        gathered = arena_b[:, 0:NGATHER * D].rearrange("p (b d) -> p b d", b=NGATHER)

        s_x = [sem(f"x_in_{t}") for t in range(T)]
        s_wq, s_wk, s_wv, s_wp, s_small = map(sem, ["wq_in", "wk_in", "wv_in", "wp_in", "small_in"])
        CTX_PIECE = 6 * P
        s_ctx = [sem(f"ctx_in_{i}") for i in range((NKEY + CTX_PIECE - 1) // CTX_PIECE)]
        s_pad = sem("pads_zeroed")
        s_ident = sem("ident_ready")
        s_var = sem("variance_ready")
        s_std = sem("std_ready")
        s_xn = sem("normed_ready")
        s_tr = sem("transposes_done")
        s_xt = sem("transposed_copied")
        s_proj = sem("projection_done")
        s_pf = sem("projection_read")
        s_kd = sem("dequantised_ready")
        s_hi = sem("high_part_ready")
        s_rest = sem("rest_ready")
        s_mid = sem("middle_part_ready")
        s_parts = sem("low_part_ready")
        s_qi = sem("query_integers_ready")
        s_qt = [sem("query_transposed_0"), sem("query_transposed_1")]
        s_kp = [sem("key_parts_stored_0"), sem("key_parts_stored_1")]
        s_vps = sem("value_product_done")
        s_vf = sem("values_copied")
        s_vmax = sem("value_maximum_done")
        s_vi = sem("value_integers_made")
        s_vb = sem("value_integers_ready")
        s_vq = sem("values_transposed")
        s_buf = sem("attention_pads_zeroed")
        s_kt = [sem(f"keys_in_{i}") for i in range(NK)]
        s_tail = sem("tail_steps_in")
        s_tout = sem("tail_outputs_in")
        s_tnorm = sem("tail_outputs_normalised")
        s_qa = sem("scores_for_max_done")
        s_qb = sem("scores_for_exp_done")
        s_max = sem("span_maximum_done")
        s_row = sem("row_maximum_done")
        s_bias = sem("exp_bias_ready")
        s_exp = sem("exp_done")
        s_conv = sem("probabilities_ready")
        s_pt = [sem("probabilities_transposed_0"), sem("probabilities_transposed_1")]
        s_av = sem("head_output_done")
        s_ao = sem("head_output_copied")
        s_attn = sem("attention_normalised")
        s_otr = sem("attention_transposes_done")
        s_ot = sem("attention_transposed_copied")
        s_out = sem("out_projection_done")
        s_x1 = sem("residual_ready")
        s_gate = sem("gate_values_ready")
        s_lg = sem("logits_done")
        s_lgc = sem("logits_centred")
        s_sc = sem("score_exps_done")
        s_sel = sem("selection_ready")
        s_pos = sem("positions_done")
        s_rows = sem("token_rows_ready")
        s_slots = sem("slots_ready")
        s_zero = sem("zeros_ready")
        s_xz = sem("expert_in_zeroed")
        s_scat = [sem(f"tokens_scattered_{j}") for j in range(TOPK)]
        s_win = [sem("weights_in_0"), sem("weights_in_1")]
        s_wready = sem("expert_weights_ready")
        s_xr = [sem("expert_rows_in_0"), sem("expert_rows_in_1")]
        s_xtr = sem("expert_rows_transposes_done")
        s_xec = sem("expert_rows_transposed_copied")
        s_h = sem("up_products_done")
        s_silu = sem("silu_done")
        s_hm = sem("hidden_ready")
        s_htr = sem("hidden_transposes_done")
        s_ht = sem("hidden_transposed_copied")
        s_y = sem("down_product_done")
        s_ya = sem("down_product_read")
        s_ys = [sem("expert_rows_out_0"), sem("expert_rows_out_1")]
        s_all_out = sem("all_expert_rows_out")
        s_gat = [sem(f"outputs_gathered_{b}") for b in range(NGATHER)]
        s_comb = sem("output_combined")
        s_store = sem("output_ready")
        s_done = sem("output_stored")
        s_dve = sem("dve_chain")
        s_act = sem("act_chain")
        s_pool = sem("pool_chain")
        s_sp = sem("sp_waits_passed")

        def rows_in(s, q):
            return 16 * (s // 2 + 1) if isinstance(s, int) else (s - q) * 8 + 16

        NV = (NKEY + BANK - 1) // BANK
        LEAD = 3
        NP = T + KT

        def spread(a, shape):
            return a.unsqueeze(2).to_broadcast(shape)

        GT = HG * (T - 1) + 1
        NTILE = NG * GT

        def tile_place(n):
            g, r = divmod(n, GT)
            return (g, None, T - 1) if r == GT - 1 else (g, g * HG + r // (T - 1), r % (T - 1))

        block = ctx.enter_context(nc.Block())

        @block.sync
        def _(sp):
            for t in range(T):
                rows = P if t < T - 1 else TAIL
                if t == T - 1:
                    sp.wait_ge(s_pad, 1)
                sp.dma_start(x_sb[0:rows, t, :], x[t * P:t * P + rows, :]).then_inc(s_x[t], 16)
                if t == 1:
                    sp.dma_start(w_qkv[:, 0, :, :], wq.rearrange("(k p) n -> p k n", p=P)).then_inc(s_wq, 16)
            sp.dma_start(bias_rows[:, 0, :], bq.unsqueeze(0).to_broadcast([P, D])).then_inc(s_small, 16)
            sp.dma_start(bias_rows[:, 1, :], bkv[0:D].unsqueeze(0).to_broadcast([P, D])).then_inc(s_small, 16)
            sp.dma_start(bias_rows[:, 2, :], bp.unsqueeze(0).to_broadcast([P, D])).then_inc(s_small, 16)
            sp.dma_start(gates[:, 0:1], g_xattn.unsqueeze(0).to_broadcast([P, 1])).then_inc(s_small, 16)
            sp.dma_start(gates[:, 1:2], g_ffn.unsqueeze(0).to_broadcast([P, 1])).then_inc(s_small, 16)
            with nc.allow_non_contiguous_dma(reason="512 words"):
                sp.dma_start(bv_col[:, :], bkv[D:2 * D].rearrange("(g p) -> p g", p=P)).then_inc(s_small, 16)
            sp.dma_start(wg_sb[:, :, :], wg_t).then_inc(s_small, 16)
            sp.dma_start(w_qkv[:, 1, :, :], wkv[:, 0:D].rearrange("(k p) n -> p k n", p=P)).then_inc(s_wk, 16)
            for i, a in enumerate(range(0, NKEY, CTX_PIECE)):
                b = min(a + CTX_PIECE, NKEY)
                sp.dma_start(ctx_sb[:, :, a:b], ctx_t[:, :, a:b]).then_inc(s_ctx[i], 16)
            sp.dma_start(w_qkv[:, 2, :, :], wkv[:, D:2 * D].rearrange("(k p) n -> p k n", p=P)).then_inc(s_wv, 16)
            for t in range(T):
                sp.wait_ge(s_qi, t + 1)
                sp.dma_start_transpose(q_t[:, :, t * P:(t + 1) * P],
                                       parts[:, t % 2].rearrange("p h g d -> p (h g d)")).then_inc(s_qt[t % 2], 16)
            with nc.allow_non_contiguous_dma(reason="single words"):
                for j in range(HG):
                    sp.dma_start(tail_step[j * HD:(j + 1) * HD, :],
                                 q_step[0:TAIL, :, T - 1].rearrange("p (g j) -> p g j", j=HG)[:, :, j]
                                 ).then_inc(s_tail, 16)
            def load_keys(head):
                sp.dma_start_transpose(k_t[head % NK].unsqueeze(1),
                                       key_parts[:, head * P:(head + 1) * P]).then_inc(s_kt[head % NK], 16)

            def transpose_values(g):
                sp.wait_ge(s_vb, g + 1)
                sp.dma_start_transpose(v_q[:, :, g * P:(g + 1) * P], v_b).then_inc(s_vq, 16)

            GROUP_AT = {NV * (g + 1) + LEAD: g for g in range(NG)}
            for kt in range(KT):
                sp.wait_ge(s_parts, kt + 1)
                sp.dma_start(key_parts[kt * P:(kt + 1) * P, :],
                             parts[:, (T + kt) % 2].rearrange("p h g d -> p (h g d)")).then_inc(s_kp[(T + kt) % 2], 16)
                if kt in GROUP_AT and kt < KT - 1:
                    transpose_values(GROUP_AT[kt])
            sp.wait_ge(s_kp[T % 2], 16 * ((KT + 1) // 2))
            sp.wait_ge(s_kp[(T + 1) % 2], 16 * (KT // 2))
            sp.wait_ge(s_proj, NP)
            load_keys(0)
            for g in range(NG - 1):
                if NV * (g + 1) + LEAD >= KT - 1:
                    transpose_values(g)
            sp.wait_ge(s_vps, NG * NV)
            load_keys(1)
            sp.dma_start(wp_sb, wp.rearrange("(k p) n -> p k n", p=P)).then_inc(s_wp, 16)

            def transpose_p(n):
                sp.wait_ge(s_conv, n + 1)
                if n >= 2:
                    sp.wait_ge(s_av, n - 1)
                sp.dma_start_transpose(p_t[n % 2], p_bf[n % 2]).then_inc(s_pt[n % 2], 16)

            for n in range(NTILE):
                g, head, t = tile_place(n)
                if n == 2:
                    transpose_values(NG - 1)
                if n >= 2:
                    transpose_p(n - 2)
                if head is not None and t == 2 and head + 2 < H:
                    if head + 2 >= NK:
                        last_tile = GT * ((head + 2 - NK) // HG + 1)
                        sp.wait_ge(s_qb, NE * last_tile)
                    load_keys(head + 2)
            for n in range(NTILE - 2, NTILE):
                transpose_p(n)

            sp.wait_ge(s_tnorm, 1)
            for j in range(HG):
                sp.dma_start(attn[0:TAIL, T - 1, :].rearrange("p (g j d) -> p g j d", g=NG, j=HG)[:, :, j, :],
                             attn_tail[j * HD:(j + 1) * HD, :, :]).then_inc(s_tout, 16)

            def load_weights(n):
                slot = n % 2
                row = n if n < EX else 0
                sp.dma_start(arena_a[:, slot * SLOT:slot * SLOT + UPC], w_up[row]).then_inc(s_win[slot], 16)
                sp.dma_start(arena_a[:, slot * SLOT + UPC:(slot + 1) * SLOT], w_down[row]).then_inc(s_win[slot], 16)

            def weights_ready(n):
                sp.wait_ge(s_win[n % 2], 32 * (n // 2 + 1))
                sp.sem_inc(s_wready, 1)

            sp.wait_ge(s_av, NTILE)

            load_weights(0)
            load_weights(1)
            weights_ready(0)
            for n in range(2, EX + 1):
                weights_ready(n - 1)
                if n - 2 < SHARED:
                    sp.wait_ge(s_y, (PRE - T, PRE)[n - 2])
                else:
                    if n - 2 == SHARED:
                        sp.wait_ge(s_slots, 1)
                    e = n - 2 - SHARED
                    sp.wait_ge(s_y, sp.value_load(end_step[0:1, e:e + 1], min_val=1, max_val=PRE + MAXT))
                    sp.sem_inc(s_sp, 1)
                load_weights(n)
            weights_ready(EX)
            for t in range(T):
                rows = P if t < T - 1 else TAIL
                sp.wait_ge(s_store, t + 1)
                sp.dma_start(out[t * P:t * P + rows, :], y_sb[0:rows, t, :]).then_inc(s_done, 16)
            sp.wait_ge(s_done, 16 * T)

        @block.tensor
        def _(pe):
            mm = nc.tensor.matmul

            def transpose_tile(src, t, done, copied, base):
                if t >= 2:
                    pe.wait_ge(copied, base + t - 1)
                for k in range(DC):
                    last = nc.tensor.transpose(ps[:, t % 2, k * P:(k + 1) * P],
                                               src[:, t, k * P:(k + 1) * P], ident[:, :])
                last.then_inc(done, 1)

            def project(j):
                if j == 0:
                    pe.wait_ge(s_wq, 16)
                if j < T:
                    pe.wait_ge(s_xt, j + 1)
                if j == T:
                    pe.wait_ge(s_wk, 16)
                if j >= T and (j - T) * P % CTX_PIECE == 0:
                    pe.wait_ge(s_ctx[(j - T) * P // CTX_PIECE], 16)
                if j >= 2:
                    pe.wait_ge(s_pf, j - 1)
                for k in range(DC):
                    src = x_t[:, k, j * P:(j + 1) * P] if j < T else ctx_sb[:, k, (j - T) * P:(j - T + 1) * P]
                    last = mm(ps[:, 2 + j % 2, :], src, w_qkv[:, 0 if j < T else 1, k, :],
                              start=(k == 0), stop=(k == DC - 1))
                last.then_inc(s_proj, 1)

            pe.wait_ge(s_ident, 1)
            for t in range(T):
                pe.wait_ge(s_xn, t + 1)
                transpose_tile(xn, t, s_tr, s_xt, 0)
                if t in (1, 2):
                    project(t - 1)
            for j in range(2, T):
                project(j)
            def make_values(v):
                g, c = divmod(v, NV)
                w = min(BANK, NKEY - c * BANK)
                if v == 0:
                    pe.wait_ge(s_wv, 16)
                if v < NV:
                    pe.wait_ge(s_ctx[(c * BANK + w - 1) // CTX_PIECE], 16)
                if v >= 2:
                    pe.wait_ge(s_vf, v - 1)
                for k in range(DC):
                    last = mm(ps[:, 4 + v % 2, 0:w], w_qkv[:, 2, k, g * P:(g + 1) * P],
                              ctx_sb[:, k, c * BANK:c * BANK + w], start=(k == 0), stop=(k == DC - 1))
                last.then_inc(s_vps, 1)

            for kt in range(KT):
                project(T + kt)
                if kt >= LEAD:
                    make_values(kt - LEAD)
            for v in range(KT - LEAD, NG * NV):
                make_values(v)

            def products(n, span, bank):
                g, head, t = tile_place(n)
                for b in range(0, span[1], BANK):
                    a, w = span[0] + b, min(BANK, span[1] - b)
                    if head is not None:
                        last = mm(ps[:, bank + b // BANK, 0:w], q_t[0:3 * HD, head, t * P:(t + 1) * P],
                                  k_t[head % NK][0:3 * HD, a:a + w], start=True, stop=True)
                    else:
                        for j in range(HG):
                            h = g * HG + j
                            last = mm(ps[j * HD:(j + 1) * HD, bank + b // BANK, 0:w],
                                      q_t[0:3 * HD, h, t * P:t * P + HD],
                                      k_t[h % NK][0:3 * HD, a:a + w], start=True, stop=True)
                return last

            def for_max(n, j):
                if not 0 <= n < NTILE:
                    return
                g, head, t = tile_place(n)
                if t == 0 and j == 0:
                    pe.wait_ge(s_kt[head % NK], 16 * (head // NK + 1))
                c = NM * n + j
                if c >= 2:
                    pe.wait_ge(s_max, c - 1)
                products(n, MAX_SPANS[j], MAX_BANK[c % 2]).then_inc(s_qa, 1)

            def for_exp(n, j):
                if not 0 <= n < NTILE:
                    return
                c = NE * n + j
                if c >= 2:
                    pe.wait_ge(s_exp, c - 1)
                products(n, EXP_SPANS[j], EXP_BANK[c % 2]).then_inc(s_qb, 1)

            def weigh_values(n):
                if not 0 <= n < NTILE:
                    return
                g, head, t = tile_place(n)
                a, w = (g * P, P) if head is None else (head * HD, HD)
                pe.wait_ge(s_pt[n % 2], 16 * (n // 2 + 1))
                if n:
                    pe.wait_ge(s_ao, n)
                for c in range(KT):
                    last = mm(ps[:, OUT_BANK, 0:w], p_t[n % 2][:, c, :], v_q[:, c, a:a + w],
                              start=(c == 0), stop=(c == KT - 1))
                last.then_inc(s_av, 1)

            pe.wait_ge(s_qt[0], 16 * ((T + 1) // 2))
            pe.wait_ge(s_qt[1], 16 * (T // 2))
            pe.wait_ge(s_vf, NG * NV)
            for_max(0, 0)
            for_max(0, 1)
            for_exp(0, 0)
            for_exp(0, 1)
            for n in range(NTILE + 4):
                if n >= 2:
                    for_exp(n - 1, 0)
                    for_exp(n - 1, 1)
                for_max(n, 2)
                for_max(n, 3)
                if n == 4:
                    pe.wait_ge(s_vq, 16 * (NG - 1))
                if n == (NG - 1) * GT + 4:
                    pe.wait_ge(s_vq, 16 * NG)
                weigh_values(n - 4)
                for_max(n + 1, 0)
                for_exp(n - 1, 2)
                for_max(n + 1, 1)

            for t in range(T):
                if t < T - 1:
                    pe.wait_ge(s_attn, t + 1)
                else:
                    pe.wait_ge(s_tout, 16 * HG)
                transpose_tile(attn, t, s_otr, s_ot, 0)
            pe.wait_ge(s_wp, 16)
            for t in range(T + 3):
                if t < T:
                    pe.wait_ge(s_ot, t + 1)
                    if t >= 2:
                        pe.wait_ge(s_x1, t - 1)
                    for k in range(DC):
                        last = mm(ps[:, 2 + t % 2, :], attn_t[:, k, t * P:(t + 1) * P], wp_sb[:, k, :],
                                  start=(k == 0), stop=(k == DC - 1))
                    last.then_inc(s_out, 1)
                if 2 <= t < T + 2:
                    if t == 2:
                        pe.wait_ge(s_ot, T)
                    pe.wait_ge(s_xn, T + t - 1)
                    transpose_tile(xn, t - 2, s_tr, s_xt, T)
                if t >= 3:
                    r = t - 3
                    pe.wait_ge(s_xt, T + r + 1)
                    for k in range(DC):
                        last = mm(ps[:, 4, r * E:(r + 1) * E], x2_t[:, k, r * P:(r + 1) * P], wg_sb[:, k, :],
                                  start=(k == 0), stop=(k == DC - 1))
            last.then_inc(s_lg, 1)

            def positions():
                pe.wait_ge(s_sel, 1)
                flat = lambda a: a.rearrange("p t e -> p (t e)")
                mm(ps[:, 0, POS:POS + T * E], upper[:, :], flat(sel[:, :, :]), start=True, stop=False)
                mm(ps[:, 0, POS:POS + T * E], ones[:, :], flat(sel_before[:, :, :]), start=False, stop=True)
                mm(ps[:, 0, TOT:TOT + E], ones[:, :], sel_total[:, :], start=True, stop=True).then_inc(s_pos, 1)

            def up(src, col, q, w):
                for k in range(DC):
                    last = mm(ps[:, 1 + 2 * q + w, 0:INTER], src(k),
                              arena_a[:, bass.ds(col + (w * DC + k) * INTER, INTER)],
                              start=(k == 0), stop=(k == DC - 1))
                return last

            def transpose_hidden(u, q):
                pe.wait_ge(s_hm, u + 1)
                if not isinstance(u, int) or u >= 1:
                    pe.wait_ge(s_ht, u)
                for c in range(IC):
                    last = nc.tensor.transpose(ps[0:IW[c], 5, c * P:(c + 1) * P],
                                               h_mul[:, q, c * P:c * P + IW[c]], ident[:, :])
                last.then_inc(s_htr, 1)

            def down(u, col, q):
                pe.wait_ge(s_ht, u + 1)
                if not isinstance(u, int) or u >= 2:
                    pe.wait_ge(s_ya, u - 1)
                for c in range(IC):
                    last = mm(ps[:, 6 + q, :], h_t[0:IW[c], q, c * P:(c + 1) * P],
                              arena_a[0:IW[c], bass.ds(col + UPC + c * D, D)], start=(c == 0), stop=(c == IC - 1))
                last.then_inc(s_y, 1)

            def transpose_rows(s, q):
                pe.wait_ge(s_xr[q], rows_in(s, q))
                if not isinstance(s, int) or s >= 1:
                    pe.wait_ge(s_xec, s)
                for k in range(DC):
                    last = nc.tensor.transpose(ps[:, 0, k * P:(k + 1) * P], x_rows[:, q, k * P:(k + 1) * P],
                                               ident[:, :])
                last.then_inc(s_xtr, 1)

            def shared(u, number, t, column_of, column_before):
                q = u % 2
                src = lambda k: x2_t[:, k, t * P:(t + 1) * P]
                if u >= 2:
                    pe.wait_ge(s_hm, number - 1)
                up(src, column_of, q, 0)
                if u:
                    transpose_hidden(number - 1, 1 - q)
                up(src, column_of, q, 1).then_inc(s_h, 1)
                if u:
                    down(number - 1, column_before, 1 - q)

            for u in range(PRE):
                part, t = shared_step(u)
                if u == POS_STEP:
                    positions()
                if u in (0, PRE - T):
                    pe.wait_ge(s_wready, part + 1)
                shared(u, u, t, part * SLOT, shared_step(max(u - 1, 0))[0] * SLOT)
            transpose_rows(0, 0)

            def column(s):
                return pe.value_load(weight_col[0:1, bass.ds(s, 1)], min_val=0, max_val=SLOT)

            def needed(s):
                return pe.value_load(weight_need[0:1, bass.ds(s, 1)], min_val=1, max_val=EX)

            def routed(s, q, col, need, col_before, look_up):
                u = PRE + s
                src = lambda k: xe_t[:, q, k, :]
                pe.wait_ge(s_wready, need)
                pe.wait_ge(s_xec, s + 1)
                pe.wait_ge(s_hm, u - 1)
                up(src, col, q, 0)
                found = look_up()
                transpose_hidden(u - 1, 1 - q)
                up(src, col, q, 1).then_inc(s_h, 1)
                transpose_rows(s + 1, 1 - q)
                down(u - 1, col_before, 1 - q)
                return found

            def pair(b, first):
                s0, s1 = b * 2, b * 2 + 1
                before = shared_step(PRE - 1)[0] * SLOT if first else column(s0 - 1)
                c0, need0 = column(s0), needed(s0)
                c1, need1 = routed(s0, 0, c0, need0, before, lambda: (column(s1), needed(s1)))
                routed(s1, 1, c1, need1, c0, lambda: None)

            pe.wait_ge(s_slots, 1)
            pairs = pe.value_load(n_pairs[0:1, 0:1], min_val=(MINT + 1) // 2, max_val=MAXT // 2)
            pair(0, True)
            with pe.Fori(1, pairs) as b:
                pair(b, False)
            last_column = column(pairs * 2 - 1)
            pe.wait_ge(s_wready, EX + 1)
            for k in range(POST):
                shared(PRE + k, pairs * 2 + PRE + k, shared_step(PRE + k)[1], (EX % 2) * SLOT,
                       (EX % 2) * SLOT if k else last_column)
            transpose_hidden(pairs * 2 + SU - 1, 1)
            down(pairs * 2 + SU - 1, (EX % 2) * SLOT, 1)

        @block.scalar
        def _(act):
            chain = [0]

            def link(ins):
                chain[0] += 1
                ins.then_inc(s_act, 1)
                act.wait_ge(s_act, chain[0])

            def copy_transposed(t, done, count, copied, dst, scale=None):
                act.wait_ge(done, count + t + 1)
                src = ps[:, t % 2, :].rearrange("p (k q) -> p k q", k=DC)
                if scale is None:
                    last = nc.scalar.copy(dst[:, :, t * P:(t + 1) * P], src)
                else:
                    for k in range(DC):
                        last = nc.scalar.activation(dst[:, k, t * P:(t + 1) * P], src[:, k, :], ACT.Copy,
                                                    scale=scale[:, k:k + 1])
                last.then_inc(copied, 1)

            def norm(n, behind, dst):
                for t in range(T + behind):
                    if t < T:
                        act.wait_ge(s_var, (n - 1) * T + t + 1)
                        nc.scalar.activation(std[:, t:t + 1], std[:, t:t + 1], ACT.Sqrt).then_inc(s_std, 1)
                    if t >= behind:
                        copy_transposed(t - behind, s_tr, (n - 1) * T, s_xt, dst)

            norm(1, 1, x_t)
            def copy_values(v):
                g, c = divmod(v, NV)
                w = min(BANK, NKEY - c * BANK)
                act.wait_ge(s_vps, v + 1)
                if c == 0 and g >= 2:
                    act.wait_ge(s_vi, g - 1)
                nc.scalar.activation(v_fs[g % 2][:, c * BANK:c * BANK + w], ps[:, 4 + v % 2, 0:w], ACT.Identity,
                                     bias=bv_col[:, g:g + 1]).then_inc(s_vf, 1)

            act.wait_ge(s_small, 16 * 7)
            for kt in range(KT):
                j = T + kt
                act.wait_ge(s_kd, kt + 1)
                if kt < 2:
                    act.wait_ge(s_qt[j % 2], 16 * ((T + 1 - j % 2) // 2))
                else:
                    act.wait_ge(s_kp[j % 2], 16 * (kt // 2))
                nc.scalar.copy(parts[:, j % 2, :, 0, :], proj_d[:, j % 2, :].rearrange("p (h d) -> p h d", h=H)
                               ).then_inc(s_hi, 1)
                if kt > LEAD:
                    copy_values(kt - LEAD - 1)
                act.wait_ge(s_rest, kt + 1)
                nc.scalar.copy(parts[:, j % 2, :, 1, :], proj_r[:, j % 2, :].rearrange("p (h d) -> p h d", h=H)
                               ).then_inc(s_mid, 1)
            for v in range(KT - LEAD - 1, NG * NV):
                copy_values(v)
            act.wait_ge(s_small, 16 * 7)
            nc.scalar.activation(gates[:, :], gates[:, :], ACT.Tanh).then_inc(s_gate, 1)

            def exps(n):
                g, head, t = tile_place(n)
                step_of, sums = ((tail_step[:, g:g + 1], tail_sums[:, g, :]) if head is None else
                                 (q_step[:, head, t:t + 1], exp_sums[:, head, t, :]))
                act.wait_ge(s_bias, n + 1)
                if n >= 2:
                    act.wait_ge(s_conv, n - 1)
                for j, (a, w) in enumerate(EXP_SPANS):
                    act.wait_ge(s_qb, NE * n + j + 1)
                    bank = BANK * EXP_BANK[(NE * n + j) % 2]
                    nc.scalar.activation(p_int[n % 2][:, a:a + w], ps_flat[:, bank:bank + w],
                                         ACT.Exp, bias=exp_bias[:, n % 2:n % 2 + 1], scale=step_of,
                                         accum_out=sums[:, j:j + 1]).then_inc(s_exp, 1)

            def keep_output(n):
                g, head, t = tile_place(n)
                act.wait_ge(s_av, n + 1)
                if head is not None:
                    last = nc.scalar.copy(attn[:, t, head * HD:(head + 1) * HD], ps[:, OUT_BANK, 0:HD])
                else:
                    for j in range(HG):
                        own = slice(j * HD, (j + 1) * HD)
                        last = nc.scalar.copy(attn_tail[own, g, :], ps[own, OUT_BANK, own])
                last.then_inc(s_ao, 1)

            act.wait_ge(s_buf, 3)
            act.wait_ge(s_tail, 16 * HG)
            for n in range(NTILE):
                exps(n)
                if n == 3:
                    act.wait_ge(s_vi, NG)
                if n >= 3:
                    keep_output(n - 3)
            for n in range(NTILE - 3, NTILE):
                keep_output(n)

            for t in range(T):
                copy_transposed(t, s_otr, 0, s_ot, attn_t, v_step)
            norm(2, 2, x2_t)
            act.wait_ge(s_lgc, 1)
            nc.scalar.activation(score[:, :, :], logit[:, :, :], ACT.Exp).then_inc(s_sc, 1)

            def silu(u, q):
                act.wait_ge(s_h, u + 1)
                nc.scalar.activation(h_act[:, q, 0:INTER], ps[:, 1 + 2 * q, 0:INTER], ACT.Silu).then_inc(s_silu, 1)

            def copy_hidden(u, q):
                act.wait_ge(s_htr, u + 1)
                for c in range(IC):
                    last = nc.scalar.copy(h_t[0:IW[c], q, c * P:(c + 1) * P], ps[0:IW[c], 5, c * P:(c + 1) * P])
                last.then_inc(s_ht, 1)

            def copy_rows(s, q):
                act.wait_ge(s_xtr, s + 1)
                nc.scalar.copy(xe_t[:, q, :, :], ps[:, 0, :].rearrange("p (k q) -> p k q", k=DC)).then_inc(s_xec, 1)

            act.wait_ge(s_xz, 16 * len(ZEROED))
            for u in range(PRE):
                if u:
                    copy_hidden(u - 1, (u - 1) % 2)
                silu(u, u % 2)
            copy_rows(0, 0)

            def routed(s, q):
                copy_hidden(PRE + s - 1, 1 - q)
                silu(PRE + s, q)
                copy_rows(s + 1, 1 - q)

            act.wait_ge(s_slots, 1)
            pairs = act.value_load(n_pairs[0:1, 0:1], min_val=(MINT + 1) // 2, max_val=MAXT // 2)
            with act.Fori(0, pairs) as b:
                for q in range(2):
                    routed(b * 2 + q, q)
            for u in range(PRE, SU):
                copy_hidden(pairs * 2 + u - 1, (u - 1) % 2)
                silu(pairs * 2 + u, u % 2)
            copy_hidden(pairs * 2 + SU - 1, 1)

        @block.vector
        def _(dve):
            v = nc.vector
            chain = [0]

            def link(ins):
                chain[0] += 1
                ins.then_inc(s_dve, 1)
                dve.wait_ge(s_dve, chain[0])

            def layer_norm(n, prepare):
                for t in range(T + 1):
                    if t < T:
                        prepare(t)
                        link(v.bn_stats(stats[:, t, :], x_sb[:, t, :]))
                        link(v.bn_aggr(mean_var[:, t, :], stats[:, t, :]))
                        v.tensor_scalar_add(std[:, t:t + 1], mean_var[:, t, 1:2], LN_EPS).then_inc(s_var, 1)
                    if t:
                        dve.wait_ge(s_std, (n - 1) * T + t)
                        link(v.reciprocal(std[:, t - 1:t], std[:, t - 1:t]))
                        v.tensor_scalar(xn[:, t - 1, :], x_sb[:, t - 1, :], mean_var[:, t - 1, 0:1],
                                        std[:, t - 1:t], ALU.subtract, ALU.mult).then_inc(s_xn, 1)

            layer_norm(1, lambda t: dve.wait_ge(s_x[t], 16))

            def bound_values(v_):
                g, c = divmod(v_, NV)
                w = min(BANK, NKEY - c * BANK)
                vals = v_fs[g % 2]
                dve.wait_ge(s_vf, v_ + 1)
                v.tensor_reduce(v_part[:, c:c + 1], vals[:, c * BANK:c * BANK + w], AX.X, ALU.max,
                                apply_absolute_value=True).then_inc(s_vmax, 1)

            def quantise_values(g):
                vals = v_fs[g % 2]
                dve.wait_ge(s_vmax, NV * (g + 1))
                link(v.tensor_reduce(v_amax[:, g:g + 1], v_part[:, :], AX.X, ALU.max))
                link(v.tensor_scalar(v_step[:, g:g + 1], v_amax[:, g:g + 1], 1.0 / 127.0, 1e-8, ALU.mult, ALU.max))
                link(v.reciprocal(v_inv[:, g:g + 1], v_step[:, g:g + 1]))
                if g:
                    dve.wait_ge(s_vq, 16 * g)
                else:
                    link(v.memset(v_i[:, NKEY:KPAD], 0))
                v.tensor_scalar(v_i[:, 0:NKEY], vals[:, 0:NKEY], v_inv[:, g:g + 1], None, ALU.mult).then_inc(s_vi, 1)
                dve.wait_ge(s_vi, g + 1)
                v.tensor_copy(v_b[:, 0:NKEY], v_i[:, 0:NKEY]).then_inc(s_vb, 1)

            dve.wait_ge(s_small, 16 * 7)
            for j in range(NP):
                b = j % 2
                kt = j - T
                pf = proj_f[:, b, :]
                heads = lambda a: a.rearrange("p (h d) -> p h d", h=H)
                dve.wait_ge(s_proj, j + 1)
                chain[0] += 1
                ins = v.tensor_tensor(pf, ps[:, 2 + b, :], bias_rows[:, 0 if j < T else 1, :], ALU.add)
                ins.then_inc(s_pf, 1)
                chain[0] -= 1
                dve.wait_ge(s_pf, j + 1)
                if j < T:
                    link(v.tensor_scalar(pf, pf, QSCALE, None, ALU.mult))
                link(v.tensor_reduce(amax[:, b, :], heads(pf), AX.X, ALU.max, apply_absolute_value=True))
                st = q_step[:, :, j] if j < T else step[:, b, :]
                link(v.tensor_scalar(st, amax[:, b, :], 1.0 / 127.0, 1e-8, ALU.mult, ALU.max))
                if j < T:
                    v.tensor_scalar(neg_q_step[:, :, j], st, -1.0, None, ALU.mult)
                link(v.reciprocal(inv_step[:, b, :], st))
                link(v.tensor_tensor(heads(proj_i[:, b, :]), heads(pf), spread(inv_step[:, b, :], [P, H, HD]), ALU.mult))
                if j < T:
                    if j >= 2:
                        dve.wait_ge(s_qt[b], 16 * (j // 2))
                    v.tensor_copy(parts[:, b].rearrange("p h g d -> p g h d"),
                                  proj_i[:, b, :].rearrange("p (h d) -> p h d", h=H).unsqueeze(1)
                                  .to_broadcast([P, HG, H, HD])).then_inc(s_qi, 1)
                else:
                    if kt >= 2:
                        dve.wait_ge(s_rest, kt - 1)
                        dve.wait_ge(s_hi, kt - 1)
                    v.tensor_tensor(heads(proj_d[:, b, :]), heads(proj_i[:, b, :]), spread(step[:, b, :], [P, H, HD]),
                                    ALU.mult).then_inc(s_kd, 1)

                if kt > LEAD:
                    v_ = kt - LEAD - 1
                    bound_values(v_)
                    if v_ % NV == NV - 1:
                        quantise_values(v_ // NV)
            for v_ in range(KT - LEAD - 1, NG * NV):
                bound_values(v_)
                if v_ % NV == NV - 1 and v_ // NV < NG - 1:
                    quantise_values(v_ // NV)

            dve.wait_ge(s_vps, NG * NV)
            for i in range(2):
                v.memset(p_int[i][:, NKEY:KPAD], 0).then_inc(s_buf, 1)
            v.memset(attn[:, T - 1, :], 0.0).then_inc(s_buf, 1)

            dve.wait_ge(s_buf, 3)
            dve.wait_ge(s_tail, 16 * HG)
            link(v.tensor_scalar(neg_tail_step[:, :], tail_step[:, :], -1.0, None, ALU.mult))

            def to_bf16(n):
                dve.wait_ge(s_exp, NE * (n + 1))
                if n >= 2:
                    dve.wait_ge(s_pt[n % 2], 16 * (n // 2))
                v.tensor_copy(p_bf[n % 2], p_int[n % 2]).then_inc(s_conv, 1)

            def maximum(n, j):
                a, w = MAX_SPANS[j]
                dve.wait_ge(s_qa, NM * n + j + 1)
                col = BANK * MAX_BANK[(NM * n + j) % 2]
                v.tensor_reduce(span_max[:, n % 2, j:j + 1], ps_flat[:, col:col + w], AX.X, ALU.max).then_inc(s_max, 1)

            for n in range(NTILE + 1):
                prev = n - 1
                if n < NTILE:
                    maximum(n, 0)
                if n:
                    dve.wait_ge(s_max, NM * n)
                    v.tensor_reduce(row_max[:, prev % 2:prev % 2 + 1], span_max[:, prev % 2, :], AX.X, ALU.max
                                    ).then_inc(s_row, 1)
                if n < NTILE:
                    maximum(n, 1)
                if n:
                    g, head, t = tile_place(prev)
                    neg_step = neg_tail_step[:, g:g + 1] if head is None else neg_q_step[:, head, t:t + 1]
                    dve.wait_ge(s_row, n)
                    if n >= 3:
                        dve.wait_ge(s_exp, NE * (prev - 1))
                    v.tensor_scalar(exp_bias[:, prev % 2:prev % 2 + 1], row_max[:, prev % 2:prev % 2 + 1],
                                    neg_step, LOG255, ALU.mult, ALU.add).then_inc(s_bias, 1)
                if n < NTILE:
                    maximum(n, 2)
                    maximum(n, 3)
                if n == 1:
                    quantise_values(NG - 1)
                if n >= 2:
                    to_bf16(n - 2)
            to_bf16(NTILE - 1)

            dve.wait_ge(s_exp, NE * NTILE)
            for inv, sums in ((inv_sum[:, :, 0:T - 1], exp_sums[:, :, 0:T - 1, :]), (tail_inv[:, :], tail_sums[:, :, :])):
                link(v.tensor_reduce(inv, sums, AX.X, ALU.add))
                link(v.reciprocal(inv, inv))
                link(v.tensor_scalar(inv, inv, 1e-8, None, ALU.max))
            dve.wait_ge(s_ao, NTILE)
            v.tensor_tensor(attn_tail, attn_tail, spread(tail_inv[:, :], [P, NG, HD]), ALU.mult).then_inc(s_tnorm, 1)
            for t in range(T - 1):
                a = attn[:, t, :].rearrange("p (h d) -> p h d", h=H)
                v.tensor_tensor(a, a, spread(inv_sum[:, :, t], [P, H, HD]), ALU.mult).then_inc(s_attn, 1)

            dve.wait_ge(s_gate, 1)
            def residual(t):
                dve.wait_ge(s_out, t + 1)
                link(v.tensor_tensor(proj_f[:, 0, :], ps[:, 2 + t % 2, :], bias_rows[:, 2, :], ALU.add))
                v.scalar_tensor_tensor(x_sb[:, t, :], proj_f[:, 0, :], gates[:, 0:1], x_sb[:, t, :],
                                       ALU.mult, ALU.add).then_inc(s_x1, 1)
                dve.wait_ge(s_x1, t + 1)

            layer_norm(2, residual)

            dve.wait_ge(s_lg, 1)
            link(v.tensor_copy(logit[:, :, :], ps[:, 4, 0:T * E].rearrange("p (t e) -> p t e", t=T)))
            link(v.tensor_reduce(tok[:, :], logit[:, :, :], AX.X, ALU.max))
            v.tensor_tensor(logit[:, :, :], logit[:, :, :], spread(tok[:, :], [P, T, E]), ALU.subtract).then_inc(s_lgc, 1)
            def compare(a, n, tmp, eq):
                shape = [P, T, n, n]
                other, own = a.unsqueeze(2).to_broadcast(shape), a.unsqueeze(3).to_broadcast(shape)
                link(v.tensor_tensor(tmp, other, own, ALU.is_gt))
                link(v.tensor_tensor(eq, other, own, ALU.is_equal))

            def ranks(dst, n, mask, tmp, eq):
                link(v.tensor_tensor(eq, eq, mask.unsqueeze(1).to_broadcast([P, T, n, n]), ALU.mult))
                link(v.tensor_tensor(tmp, tmp, eq, ALU.add))
                link(v.tensor_reduce(dst, tmp, AX.X, ALU.add))

            def choose_groups():
                dve.wait_ge(s_sc, 1)
                link(v.tensor_reduce(tok[:, :], score[:, :, :], AX.X, ALU.add))
                link(v.reciprocal(tok[:, :], tok[:, :]))
                link(v.tensor_tensor(score[:, :, :], score[:, :, :], spread(tok[:, :], [P, T, E]), ALU.mult))
                link(v.tensor_reduce(grp[:, :, :], score[:, :, :].rearrange("p t (g e) -> p t g e", g=EG), AX.X, ALU.max))

                small = lambda a: a.rearrange("p t e f -> p (t e f)")[:, 0:T * EG * EG].rearrange(
                    "p (t e f) -> p t e f", t=T, e=EG)
                dve.wait_ge(s_pool, 8)
                dve.wait_ge(s_av, NTILE)
                compare(grp[:, :, :], EG, small(rank_tmp), small(rank_eq))
                ranks(grp_rank[:, :, :], EG, before_g[:, :, :], small(rank_tmp), small(rank_eq))
                link(v.tensor_scalar(grp[:, :, :], grp_rank[:, :, :], TOPG - 0.5, None, ALU.is_lt))
                link(v.tensor_scalar(grp_rank[:, :, :], grp[:, :, :], -1.0, None, ALU.add))
                by_group = lambda a: a.rearrange("p t (g e) -> p t g e", g=EG)
                gs = [P, T, EG, E // EG]
                link(v.tensor_tensor(by_group(logit[:, :, :]), by_group(score[:, :, :]),
                                     grp[:, :, :].unsqueeze(3).to_broadcast(gs), ALU.mult))
                link(v.tensor_tensor(by_group(logit[:, :, :]), by_group(logit[:, :, :]),
                                     grp_rank[:, :, :].unsqueeze(3).to_broadcast(gs), ALU.add))

            def compare_experts():
                compare(logit[:, :, :], E, rank_tmp, rank_eq)

            def rank_experts():
                ranks(rank[:, :, :], E, before[:, :, :], rank_tmp, rank_eq)

            def select():
                link(v.tensor_scalar(sel[:, :, :], rank[:, :, :], TOPK - 0.5, None, ALU.is_lt))
                link(v.tensor_scalar(sel[:, T - 1, :], sel[:, T - 1, :], valid[:, 0:1], None, ALU.mult))
                link(v.memset(sel_before[:, 0, :], 0.0))
                for t in range(1, T):
                    link(v.tensor_tensor(sel_before[:, t, :], sel_before[:, t - 1, :], sel[:, t - 1, :], ALU.add))
                v.tensor_tensor(sel_total[:, :], sel_before[:, T - 1, :], sel[:, T - 1, :], ALU.add).then_inc(s_sel, 1)

            def weigh_ranks():
                for j in range(TOPK):
                    link(v.scalar_tensor_tensor(pick[:, :, :], rank[:, :, :], float(j), score[:, :, :],
                                                ALU.is_equal, ALU.mult))
                    link(v.tensor_reduce(weight_j[:, j, :], pick[:, :, :], AX.X, ALU.add))

            def place_tokens():
                dve.wait_ge(s_pos, 1)
                link(v.tensor_copy(count[:, :], ps[:, 0, TOT:TOT + E]))
                shape = [P, E, T - 1]
                link(v.tensor_tensor(over[:, :, :], count[:, :].unsqueeze(2).to_broadcast(shape),
                                     thresholds[:, :].unsqueeze(1).to_broadcast(shape), ALU.is_gt))
                link(v.tensor_reduce(tiles_of[:, :], over[:, :, :], AX.X, ALU.add))
                link(v.tensor_scalar(tiles_of[:, :], tiles_of[:, :], 1.0, None, ALU.add))
                link(v.tensor_tensor(prefix[:, :, :], before[:, :, :],
                                     tiles_of[:, :].unsqueeze(1).to_broadcast([P, E, E]), ALU.mult))
                link(v.tensor_reduce(first_tile[:, :], prefix[:, :, :], AX.X, ALU.add))
                link(v.tensor_tensor(end_tile[:, :], first_tile[:, :], tiles_of[:, :], ALU.add))
                link(v.tensor_scalar(end_step[:, :], end_tile[:, :], float(PRE), None, ALU.add))
                for less in range(2):
                    link(v.tensor_scalar(n_pairs[:, less:less + 1], end_tile[:, E - 1:E], 0.5, 0.25 - less,
                                         ALU.mult, ALU.add))
                link(v.tensor_scalar(first_tile[:, :], first_tile[:, :], float(P), None, ALU.mult))
                link(v.tensor_tensor(slot_of[:, :, :], ps[:, 0, POS:POS + T * E].rearrange("p (t e) -> p t e", t=T),
                                     first_tile[:, :].unsqueeze(1).to_broadcast([P, T, E]), ALU.add))
                for j in range(TOPK):
                    link(v.scalar_tensor_tensor(pick[:, :, :], rank[:, :, :], float(j), slot_of[:, :, :],
                                                ALU.is_equal, ALU.mult))
                    link(v.tensor_reduce(slot_j[:, j, :], pick[:, :, :], AX.X, ALU.add))
                v.tensor_copy(slot_i[:, :, :], slot_j[:, :, :]).then_inc(s_rows, 1)

            def place_weights():
                shape = [P, MAXT, E]
                link(v.tensor_tensor(past[:, :, :], end_tile[:, :].unsqueeze(1).to_broadcast(shape),
                                     tile_no[:, :].unsqueeze(2).to_broadcast(shape), ALU.is_le))
                link(v.tensor_reduce(tile_expert[:, :], past[:, :, :], AX.X, ALU.add))
                link(v.tensor_scalar(tile_expert[:, :], tile_expert[:, :], float(E - 1), None, ALU.min))
                link(v.tensor_scalar(weight_need[:, :], tile_expert[:, :], float(SHARED + 1), None, ALU.add))
                link(v.tensor_scalar(weight_col[:, :], tile_expert[:, :], 0.5, -0.25, ALU.mult, ALU.add))
                link(v.tensor_scalar(tile_tmp[:, :], weight_col[:, :], -2.0, None, ALU.mult))
                link(v.tensor_tensor(tile_tmp[:, :], tile_tmp[:, :], tile_expert[:, :], ALU.add))
                v.tensor_scalar(weight_col[:, :], tile_tmp[:, :], float(SLOT), None, ALU.mult).then_inc(s_slots, 1)

            def gate(u, q):
                dve.wait_ge(s_silu, u + 1)
                if not isinstance(u, int) or u >= 2:
                    dve.wait_ge(s_htr, u - 1)
                v.tensor_tensor(h_mul[:, q, 0:INTER], ps[:, 2 + 2 * q, 0:INTER], h_act[:, q, 0:INTER],
                                ALU.mult).then_inc(s_hm, 1)

            def keep_shared(u, number):
                part, t = shared_step(u)
                dve.wait_ge(s_y, number + 1)
                if u < PRE and (part == 0 or t >= PRE - T):
                    v.tensor_copy(y_sb[:, t, :], ps[:, 6 + u % 2, :]).then_inc(s_ya, 1)
                else:
                    dve.wait_ge(s_ya, number)
                    v.tensor_tensor(y_sb[:, t, :], ps[:, 6 + u % 2, :], y_sb[:, t, :], ALU.add).then_inc(s_ya, 1)

            def keep_routed(s, q, stored):
                dve.wait_ge(s_y, PRE + s + 1)
                if stored is not None:
                    dve.wait_ge(s_ys[q], stored)
                v.tensor_copy(y_rows[:, q, :], ps[:, 6 + (PRE + q) % 2, :]).then_inc(s_ya, 1)

            choose_groups()
            for u in range(PRE):
                gate(u, u % 2)
                if u:
                    keep_shared(u - 1, u - 1)
                if u == 0:
                    compare_experts()
                if u == 1:
                    rank_experts()
                    select()
                if u == POS_STEP - 1:
                    place_tokens()
                if u == POS_STEP:
                    place_weights()
                    weigh_ranks()
            gate(PRE, 0)
            keep_shared(PRE - 1, PRE - 1)
            gate(PRE + 1, 1)
            keep_routed(0, 0, None)
            pairs = dve.value_load(n_pairs[0:1, 0:1], min_val=(MINT + 1) // 2, max_val=MAXT // 2)
            before_last = dve.value_load(n_pairs[0:1, 1:2], min_val=(MINT + 1) // 2 - 1, max_val=MAXT // 2 - 1)

            def keep_pair(b, first):
                gate(PRE + b * 2, 0)
                keep_routed(b * 2 - 1, 1, None if first else (b - 1) * 16)
                gate(PRE + b * 2 + 1, 1)
                keep_routed(b * 2, 0, b * 16)

            keep_pair(1, True)
            with dve.Fori(2, pairs) as b:
                keep_pair(b, False)

            def combine(t):
                rows = P if t < T - 1 else TAIL
                for j in range(TOPK):
                    n = t * TOPK + j
                    dve.wait_ge(s_gat[n % NGATHER], 16 * (n // NGATHER + 1))
                    if j:
                        dve.wait_ge(s_comb, n)
                    v.scalar_tensor_tensor(y_sb[0:rows, t, :], gathered[0:rows, n % NGATHER, :],
                                           weight_j[0:rows, j, t:t + 1], y_sb[0:rows, t, :],
                                           ALU.mult, ALU.add).then_inc(s_comb, 1)
                dve.wait_ge(s_comb, (t + 1) * TOPK)
                v.scalar_tensor_tensor(y_sb[0:rows, t, :], y_sb[0:rows, t, :], gates[0:rows, 1:2],
                                       x_sb[0:rows, t, :], ALU.mult, ALU.add).then_inc(s_store, 1)

            for u in range(PRE, SU):
                gate(pairs * 2 + u, u % 2)
                if u == PRE:
                    keep_routed(pairs * 2 - 1, 1, before_last * 16)
                else:
                    keep_shared(u - 1, pairs * 2 + u - 1)
                if COMBINED[u - PRE]:
                    dve.wait_ge(s_ya, pairs * 2 + u)
                for t in COMBINED[u - PRE]:
                    combine(t)
            keep_shared(SU - 1, pairs * 2 + SU - 1)
            dve.wait_ge(s_ya, pairs * 2 + SU)
            for t in COMBINED[POST]:
                combine(t)

        @block.gpsimd
        def _(pool):
            p = nc.gpsimd
            p.memset(x_sb[:, T - 1, :], 0.0).then_inc(s_pad, 1)
            p.memset(ctx_sb[:, :, NKEY:KPAD], 0.0).then_inc(s_pool, 1)
            p.memset(ident[:, :], 0.0).then_inc(s_pool, 1)
            pool.wait_ge(s_pool, 2)
            p.affine_select(out=ident[:, :], in_=ident[:, :], compare_op=ALU.not_equal, fill=1.0, base=0,
                            pattern=[[-1, P]], channel_multiplier=1).then_inc(s_ident, 1)
            p.memset(before[:, :, :], 1.0).then_inc(s_pool, 1)
            pool.wait_ge(s_pool, 3)
            p.affine_select(out=before[:, :, :], in_=before[:, :, :], compare_op=ALU.is_gt, fill=0.0, base=0,
                            pattern=[[1, E], [-1, E]], channel_multiplier=0).then_inc(s_pool, 1)
            p.memset(before_g[:, :, :], 1.0).then_inc(s_ident, 1)
            pool.wait_ge(s_ident, 2)
            p.affine_select(out=before_g[:, :, :], in_=before_g[:, :, :], compare_op=ALU.is_gt, fill=0.0, base=0,
                            pattern=[[1, EG], [-1, EG]], channel_multiplier=0).then_inc(s_pool, 1)
            p.memset(ones[:, :], 1.0).then_inc(s_pool, 1)
            pool.wait_ge(s_pool, 6)
            p.affine_select(out=upper[:, :], in_=ones[:, :], compare_op=ALU.is_gt, fill=0.0, base=0,
                            pattern=[[1, P]], channel_multiplier=-1).then_inc(s_pool, 1)
            p.affine_select(out=valid[:, :], in_=ones[:, 0:1], compare_op=ALU.is_gt, fill=0.0, base=TAIL,
                            pattern=[[0, 1]], channel_multiplier=-1).then_inc(s_zero, 1)
            p.iota(iota_i[:, :], [[1, MAXT]], base=0, channel_multiplier=0).then_inc(s_zero, 1)
            pool.wait_ge(s_zero, 2)
            p.tensor_copy(tile_no[:, :], iota_i[:, :]).then_inc(s_zero, 1)
            pool.wait_ge(s_zero, 3)
            p.tensor_scalar(thresholds[:, :], tile_no[:, 1:T], float(P), None, ALU.mult).then_inc(s_pool, 1)
            for kt in range(KT):
                j = T + kt
                b = j % 2
                heads = lambda a: a.rearrange("p (h d) -> p h d", h=H)
                pool.wait_ge(s_kd, kt + 1)
                pool.wait_ge(s_hi, kt + 1)
                p.tensor_tensor(heads(proj_r[:, b, :]), heads(proj_d[:, b, :]), parts[:, b, :, 0, :],
                                ALU.subtract).then_inc(s_rest, 1)
                pool.wait_ge(s_rest, kt + 1)
                pool.wait_ge(s_mid, kt + 1)
                p.tensor_tensor(parts[:, b, :, 2, :], heads(proj_r[:, b, :]), parts[:, b, :, 1, :],
                                ALU.subtract).then_inc(s_parts, 1)

            pool.wait_ge(s_mid, KT)
            pool.wait_ge(s_parts, KT)
            p.memset(proj_r[:, 0, :], 0.0).then_inc(s_zero, 1)
            pool.wait_ge(s_zero, 4)
            for i, (rows, a) in enumerate(ZEROED):
                pool.wait_ge(s_conv, i + 8)
                pool.dma_start(rows[a * P:(a + 1) * P, :], proj_r[:, 0, :]).then_inc(s_xz, 16)

            pool.wait_ge(s_rows, 1)
            pool.wait_ge(s_xz, 16 * len(ZEROED))
            for n in range(T * TOPK):
                t, j = divmod(n, TOPK)
                rows = P if t < T - 1 else TAIL
                p.indirect_dma_start(out=expert_in,
                                     out_offset=bass.IndirectOffsetOnAxis(ap=slot_i[0:rows, j, t:t + 1], axis=0),
                                     in_=xn[0:rows, t, :], in_offset=None).then_inc(s_scat[j], 16)
            for j in range(TOPK):
                pool.wait_ge(s_scat[j], 16 * T)

            def load_rows(s, q):
                pool.dma_start(x_rows[:, q, :], expert_in[bass.ds(s * P, P), :]).then_inc(s_xr[q], 16)

            def store_rows(s, q):
                pool.wait_ge(s_ya, PRE + s + 1)
                pool.dma_start(expert_out[bass.ds(s * P, P), :], y_rows[:, q, :]).then_inc(s_ys[q], 16)

            load_rows(0, 0)
            load_rows(1, 1)
            pool.wait_ge(s_slots, 1)
            pairs = pool.value_load(n_pairs[0:1, 0:1], min_val=(MINT + 1) // 2, max_val=MAXT // 2)

            def move_pair(b, first):
                for q in range(2):
                    pool.wait_ge(s_xtr, b * 2 + q + 1)
                    load_rows(b * 2 + q + 2, q)
                    if not first:
                        store_rows(b * 2 + q - 2, q)

            move_pair(0, True)
            with pool.Fori(1, pairs) as b:
                move_pair(b, False)
            for q in range(2):
                store_rows(pairs * 2 - 2 + q, q)
            for q in range(2):
                pool.wait_ge(s_ys[q], pairs * 16)
                pool.sem_inc(s_all_out, 1)
            for n in range(T * TOPK):
                t, j = divmod(n, TOPK)
                rows = P if t < T - 1 else TAIL
                if n >= NGATHER:
                    pool.wait_ge(s_comb, n - NGATHER + 1)
                p.indirect_dma_start(out=gathered[0:rows, n % NGATHER, :], out_offset=None, in_=expert_out,
                                     in_offset=bass.IndirectOffsetOnAxis(ap=slot_i[0:rows, j, t:t + 1], axis=0)
                                     ).then_inc(s_gat[n % NGATHER], 16)


def kernel(**inputs):
    import numpy as _np
    import concourse.bacc as _bacc
    from concourse import mybir as _mybir
    from concourse.bass_utils import run_bass_kernel_spmd as _run

    P = 128
    a = {k: _np.asarray(v) for k, v in inputs.items()}
    x, ctx = a["x"], a["ctx_2048"]
    D = x.shape[-1]
    DC = D // P
    w1, w3, w2 = a["L0_ffn_W1"], a["L0_ffn_W3"], a["L0_ffn_W2"]
    E, I = w1.shape[:2]
    s1 = a["L0_ffn_Ws1"].reshape(-1, I, D)
    s3 = a["L0_ffn_Ws3"].reshape(-1, I, D)
    s2 = a["L0_ffn_Ws2"].reshape(D, -1, I).transpose(1, 0, 2)
    IC = (I + P - 1) // P

    def up(w):
        return w.reshape(-1, I, DC, P).transpose(0, 3, 2, 1)

    def down(w):
        full = _np.zeros((w.shape[0], IC * P, D), w.dtype)
        full[:, :I] = w.transpose(0, 2, 1)
        return full.reshape(-1, IC, P, D).transpose(0, 2, 1, 3)

    ups = _np.stack([_np.concatenate([up(s1), up(w1)]), _np.concatenate([up(s3), up(w3)])], axis=2)
    downs = _np.concatenate([down(s2), down(w2)])
    laid = {
        "x": x.reshape(-1, D),
        "ctx_t": ctx.reshape(-1, DC, P).transpose(2, 1, 0),
        "g_xattn": a["g_xattn"],
        "g_ffn": a["g_ffn"],
        "wq": a["L0_xattn_Wq"],
        "bq": a["L0_xattn_bq"],
        "wkv": a["L0_xattn_Wkv"],
        "bkv": a["L0_xattn_bkv"],
        "wp": a["L0_xattn_Wp"],
        "bp": a["L0_xattn_bp"],
        "wg_t": a["L0_ffn_Wg"].reshape(E, DC, P).transpose(2, 1, 0),
        "w_up": ups.reshape(ups.shape[0], P, -1),
        "w_down": downs.reshape(downs.shape[0], P, -1),
    }
    laid = {k: _np.ascontiguousarray(v) for k, v in laid.items()}
    nc = _bacc.Bacc("TRN2", target_bir_lowering=False, num_devices=1)
    args = [nc.dram_tensor(f"in_{k}", v.shape, _mybir.dt.from_np(v.dtype), kind="ExternalInput").ap()
            for k, v in laid.items()]
    args.append(nc.dram_tensor("out_0", laid["x"].shape, _mybir.dt.float32, kind="ExternalOutput").ap())
    gated_xattn_moe_kernel(nc, *args)
    r = _run(nc, [{f"in_{k}": v for k, v in laid.items()}], core_ids=[0])
    return r.results[0]["out_0"].reshape(x.shape)
```
